# Optimizing a Trainium2 kernel written in Bass

```python
import numpy as np
import jax
import jax.numpy as jnp

def _softmax(x, axis=-1):
    return jax.nn.softmax(x, axis=axis)

def _gelu(x):
    return jax.nn.gelu(x, approximate=True)

def _silu(x):
    return jax.nn.silu(x)

def _sigmoid(x):
    return jax.nn.sigmoid(x)

def _layernorm(x, axis=-1, eps=1e-05):
    m = jnp.mean(x, axis=axis, keepdims=True)
    v = jnp.var(x, axis=axis, keepdims=True)
    return (x - m) / jnp.sqrt(v + eps)

def _scatter_add(tgt, idx, src, axis=0):
    return tgt.at[idx].add(src)

def _segment_sum(src, seg, n):
    return jax.ops.segment_sum(src, seg, n)
kernel_name = 'mk_gnn_ffn_d1_gnn_r8_647cb0'

def setup_inputs(seed: int=0):
    np.random.seed(seed)
    _w = jnp.asarray

    def _rec_inputs():
        import jax
        import jax.numpy as jnp
        _gk = jax.random.key(seed)
        x = -0.0003713 + 1 * jax.random.normal(jax.random.fold_in(_gk, 1), (6250, 256), jnp.float32)
        src = jax.random.randint(jax.random.fold_in(_gk, 2), (100000,), 0, 6250, jnp.int32)
        dst = jnp.minimum((6250 * jax.random.uniform(jax.random.fold_in(_gk, 3), (100000,)) ** 2.0).astype(jnp.int32), 49999)
        _o = jnp.argsort(dst, stable=True)
        src = src[_o]
        dst = dst[_o]
        return (x, src, dst)
    x, src, dst = _rec_inputs()

    def _L0_gnn_setup():
        import jax, jax.numpy as jnp
        import numpy as np
        N_NODES = 6250
        N_EDGES = 100000
        D_IN = 256
        D_HID = 256
        D_OUT = 256
        key = jax.random.key(seed)
        k_x, k_e, k_w1, k_wm = jax.random.split(key, 4)
        input_matrix = jax.random.normal(k_x, (N_NODES, D_IN), dtype=jnp.float32)
        adjacency_coo_matrix = jax.random.randint(k_e, (2, N_EDGES), 0, N_NODES, dtype=jnp.int32)
        fc_w = jax.random.normal(k_w1, (D_IN, D_HID), dtype=jnp.float32) * (1.0 / np.sqrt(D_IN))
        fc_b = jnp.zeros((D_HID,), dtype=jnp.float32)
        lim = np.sqrt(6.0 / (D_IN + D_HID + D_OUT)).astype(np.float32)
        weights_matrix = jax.random.uniform(k_wm, (D_IN + D_HID, D_OUT), dtype=jnp.float32, minval=-lim, maxval=lim)
        return {'input_matrix': input_matrix, 'adjacency_coo_matrix': adjacency_coo_matrix, 'fc_w': fc_w, 'fc_b': fc_b, 'weights_matrix': weights_matrix}
    _L0_gnn_all = _L0_gnn_setup()
    _L0_gnn_in = {k: v for k, v in _L0_gnn_all.items() if k in ('fc_w', 'fc_b', 'weights_matrix')}
    del _L0_gnn_all

    def _L0_ffn_setup():
        import jax, jax.numpy as jnp
        import numpy as np
        TOP_K = 2
        LN_EPS = 1e-05
        key = jax.random.key(seed)
        ks = jax.random.split(key, 8)
        B, S, D, E, H = (16, 1024, 256, 8, 1024)
        x = jax.random.normal(ks[0], (B, S, D), dtype=jnp.float32)
        Wr = jax.random.normal(ks[1], (D, E), dtype=jnp.float32) * 0.1
        br = jnp.zeros((E,), dtype=jnp.float32)
        ln_g = jnp.ones((E, D), dtype=jnp.float32)
        ln_b = jnp.zeros((E, D), dtype=jnp.float32)
        W1 = jax.random.normal(ks[2], (E, D, H), dtype=jnp.float32) * (1.0 / np.sqrt(D))
        b1 = jnp.zeros((E, H), dtype=jnp.float32)
        W2 = jax.random.normal(ks[3], (E, H, D), dtype=jnp.float32) * (1.0 / np.sqrt(H))
        b2 = jnp.zeros((E, D), dtype=jnp.float32)
        return {'x': x, 'Wr': Wr, 'br': br, 'ln_g': ln_g, 'ln_b': ln_b, 'W1': W1, 'b1': b1, 'W2': W2, 'b2': b2}
    _L0_ffn_all = _L0_ffn_setup()
    _L0_ffn_in = {k: v for k, v in _L0_ffn_all.items() if k in ('Wr', 'br', 'ln_g', 'ln_b', 'W1', 'b1', 'W2', 'b2')}
    del _L0_ffn_all
    return {'x': x, 'src': src, 'dst': dst, 'L0_gnn_fc_w': _L0_gnn_in['fc_w'], 'L0_gnn_fc_b': _L0_gnn_in['fc_b'], 'L0_gnn_weights_matrix': _L0_gnn_in['weights_matrix'], 'L0_ffn_Wr': _L0_ffn_in['Wr'], 'L0_ffn_br': _L0_ffn_in['br'], 'L0_ffn_ln_g': _L0_ffn_in['ln_g'], 'L0_ffn_ln_b': _L0_ffn_in['ln_b'], 'L0_ffn_W1': _L0_ffn_in['W1'], 'L0_ffn_b1': _L0_ffn_in['b1'], 'L0_ffn_W2': _L0_ffn_in['W2'], 'L0_ffn_b2': _L0_ffn_in['b2']}

def reference(x, src, dst, L0_gnn_fc_w, L0_gnn_fc_b, L0_gnn_weights_matrix, L0_ffn_Wr, L0_ffn_br, L0_ffn_ln_g, L0_ffn_ln_b, L0_ffn_W1, L0_ffn_b1, L0_ffn_W2, L0_ffn_b2):
    import jax
    import jax.numpy as jnp

    def _L0_gnn_ref(input_matrix, adjacency_coo_matrix, fc_w, fc_b, weights_matrix):
        import jax, jax.numpy as jnp
        import numpy as np
        N_NODES = 6250
        N_EDGES = 100000
        D_IN = 256
        D_HID = 256
        D_OUT = 256
        n_nodes = input_matrix.shape[0]
        edge_src = adjacency_coo_matrix[0]
        edge_trg = adjacency_coo_matrix[1]
        neighbors = input_matrix[edge_trg]
        neighbors_repr = jax.nn.relu(neighbors @ fc_w + fc_b)
        aggregated = jax.ops.segment_max(neighbors_repr, edge_src, num_segments=n_nodes)
        aggregated = jnp.maximum(aggregated, 0.0)
        concat = jnp.concatenate([input_matrix, aggregated], axis=1)
        return concat @ weights_matrix

    def _L0_ffn_ref(x, Wr, br, ln_g, ln_b, W1, b1, W2, b2):
        import jax, jax.numpy as jnp
        import numpy as np
        TOP_K = 2
        LN_EPS = 1e-05
        B, S, D = x.shape
        N = B * S
        xt = x.reshape(N, D)
        logits = xt @ Wr + br
        probs = jax.nn.softmax(logits, axis=-1)
        top_p, top_idx = jax.lax.top_k(probs, TOP_K)
        weights = top_p / top_p.sum(axis=-1, keepdims=True)
        mu = xt.mean(axis=-1, keepdims=True)
        var = ((xt - mu) ** 2).mean(axis=-1, keepdims=True)
        xn = (xt - mu) * jax.lax.rsqrt(var + LN_EPS)
        xe = xn[None, :, :] * ln_g[:, None, :] + ln_b[:, None, :]
        h = jax.nn.gelu(jnp.einsum('end,edh->enh', xe, W1) + b1[:, None, :], approximate=False)
        y = jnp.einsum('enh,ehd->end', h, W2) + b2[:, None, :]
        y_tok = jnp.transpose(y, (1, 0, 2))
        sel = jnp.take_along_axis(y_tok, top_idx[:, :, None], axis=1)
        out = (weights[:, :, None] * sel).sum(axis=1)
        return out.reshape(B, S, D)
    edge_index = jnp.stack([src, dst])
    x = x + _L0_gnn_ref(_layernorm(x, axis=-1), edge_index, L0_gnn_fc_w, L0_gnn_fc_b, L0_gnn_weights_matrix)
    x = x + _L0_ffn_ref(_layernorm(x, axis=-1)[None], L0_ffn_Wr, L0_ffn_br, L0_ffn_ln_g, L0_ffn_ln_b, L0_ffn_W1, L0_ffn_b1, L0_ffn_W2, L0_ffn_b2)[0]
    return x

_drawn_inputs = setup_inputs


def setup_inputs(seed=0):
    import zlib

    import numpy as np

    out = dict(_drawn_inputs(seed))
    spreads = {'L0_gnn_fc_b': (0.0, 0.1),
     'L0_ffn_br': (0.0, 0.1),
     'L0_ffn_ln_g': (1.0, 0.2),
     'L0_ffn_ln_b': (0.0, 0.312),
     'L0_ffn_b1': (0.0, 0.306),
     'L0_ffn_b2': (0.0, 0.1)}
    factors = {}
    for name, (base, spread) in spreads.items():
        noise = np.random.default_rng([zlib.crc32(name.encode()), seed]).standard_normal(out[name].shape)
        drawn = base * np.exp(spread * noise) if base else spread * noise
        out[name] = jnp.asarray(drawn.astype(out[name].dtype))
    for name, factor in factors.items():
        out[name] = (out[name] * factor).astype(out[name].dtype)
    return out
```

```python
from contextlib import ExitStack

import concourse.bass as bass
from concourse import mybir

F32 = mybir.dt.float32
F16 = mybir.dt.float16
BF16 = mybir.dt.bfloat16
I32 = mybir.dt.int32
ALU = mybir.AluOpType
ACT = mybir.ActivationFunctionType
AX = mybir.AxisListType

P = 128
N_NODES = 6250
N_EDGES = 100000
D = 256
DC = D // P
E = 8
H = 1024
HC = H // P
EPS = 1e-5

NT = -(-N_NODES // P)
G = 7
NG = NT // G
TAIL = N_NODES - (NT - 1) * P

SORT_F = 1024
SRC_P, SRC_F = 125, 800
DST_BITS = 13
LEVELS = 17
FREE_LEVELS = 10
W = -(-N_EDGES // P)
HALF = 17
GTURNS = W // (2 * HALF)
ZERO_ROW = W * P

FT = 256
SUB = FT // P
REGION = 6528
EARLY = 4
FTILES = (2 * N_NODES + E * (FT - 1)) // FT
SLOT_ROWS = E * REGION + FT + 2 * P
TRASH = E * REGION + FT
ROW = D + 2
ACC_PAD = NT * P
ACC_ROWS = ACC_PAD + P
WS = 64.0
XB = 4

PK_W = 2 * (DC * H + HC * D) // 2
PK_G = PK_W
PK_B = PK_G + DC
PK_B1 = PK_B + DC
PK_B2 = PK_B1 + HC
PACK = PK_B2 + D
PARAMS = PACK - PK_W

assert NG * G == NT and GTURNS * 2 * HALF == W and SRC_P * SRC_F == N_EDGES
assert FTILES % XB == 0 and 2 * E <= GTURNS

C_IDENT = 0
C_TRI = C_IDENT + P
C_ONES = C_TRI + P
C_IOTA = C_ONES + P
C_SIGN = C_IOTA + P
C_EXP = C_SIGN + LEVELS - FREE_LEVELS + 1
C_EBASE = C_EXP + G * E
C_VALID = C_EBASE + G * E
C_TRASH = C_VALID + NT
C_TRASH2 = C_TRASH + NT
C_TOKEN = C_TRASH2 + NT
C_TILE = C_TOKEN + NT
C_PADID = C_TILE + FTILES
C_ALL = C_PADID + 1


EDGE_STEPS = 13
TAB_STEPS = 21
CR_DIAG = 3
CR_DONE = 10
FTAB_STEPS = 28
RANK_AT = 14
EXP_AT = 15
ROUTE_STEPS = 39
SORT_TURN_AT = []
_n = 4 + FREE_LEVELS * (FREE_LEVELS + 1)
for _m in range(1, LEVELS - FREE_LEVELS + 1):
    SORT_TURN_AT += [_n + 1, _n + 1 + 2 * _m]
    _n = SORT_TURN_AT[-1] + 2 * FREE_LEVELS
SORT_DONE = _n
_flips = FREE_LEVELS * (FREE_LEVELS + 1) // 2
SORT_TURN_FROM = []
for _m in range(1, LEVELS - FREE_LEVELS + 1):
    SORT_TURN_FROM += [(_flips + 1) % 2, (_flips + 1 + 1 + _m) % 2]
    _flips += 1 + 1 + _m + 1 + FREE_LEVELS
SORT_ENDS_IN = _flips % 2


_late = [divmod(_t, G) for _t in range(EARLY * G, NT)]
_each = -(-len(_late) // (LEVELS - FREE_LEVELS))
LATE_TILES = [_late[_m * _each:(_m + 1) * _each] for _m in range(LEVELS - FREE_LEVELS)]


def constants():
    import numpy as np

    c = np.zeros((P, C_ALL), np.float32)
    p = np.arange(P)
    c[:, C_IDENT:C_IDENT + P] = np.eye(P)
    c[:, C_TRI:C_TRI + P] = p[:, None] < p[None, :]
    c[:, C_ONES:C_ONES + P] = 1
    c[:, C_IOTA:C_IOTA + P] = p[None, :]
    sign = [1 - 2 * ((p >> (lv - FREE_LEVELS)) & 1) for lv in range(FREE_LEVELS, LEVELS + 1)]
    c[:, C_SIGN] = sign[0]
    for j in range(1, len(sign)):
        c[:, C_SIGN + j] = sign[j - 1] * sign[j]
    c[:, C_EXP:C_EXP + G * E] = np.tile(np.arange(E), G)
    c[:, C_EBASE:C_EBASE + G * E] = np.tile(np.arange(E) * REGION, G)
    node = np.arange(NT)[None, :] * P + p[:, None]
    c[:, C_VALID:C_VALID + NT] = node < N_NODES
    c[:, C_TRASH:C_TRASH + NT] = (node >= N_NODES) * (TRASH + p[:, None])
    c[:, C_TRASH2:C_TRASH2 + NT] = (node >= N_NODES) * (TRASH + P + p[:, None])
    c[:, C_TOKEN:C_TOKEN + NT] = node
    c[:, C_TILE:C_TILE + FTILES] = np.arange(FTILES)
    c[:, C_PADID] = ACC_PAD + p
    return c


def gnn_moe_kernel(nc, x, src, dst, fc, fc_b, w_bot, wr, br, params, w1, w2, const, out, scratch_kind="Internal"):
    ctx = ExitStack()
    with ctx:
        def sb(name, shape, dt=F32):
            return ctx.enter_context(nc.sbuf_tensor(name, shape, dt))

        def sem(name):
            return ctx.enter_context(nc.semaphore(name))

        def dram(name, shape, dt=F32):
            return nc.dram_tensor(name, shape, dt, kind=scratch_kind).ap()

        h_dram = dram("h_rows", [NT * P, D])
        key_dram = dram("sorted_keys", [P * SORT_F])
        hist = dram("history", [ZERO_ROW + 1, D])
        slots = dram("slots", [SLOT_ROWS, ROW])
        acc = dram("acc", [ACC_ROWS, D])
        packs = dram("packs", [E, P, PACK])

        bank = [ctx.enter_context(nc.psum_tensor(f"bank{i}", [P, 512], F32)) for i in range(8)]

        cst = sb("cst", [P, C_ALL])
        ident = cst[:, C_IDENT:C_IDENT + P]
        tri = cst[:, C_TRI:C_TRI + P]
        ones = cst[:, C_ONES:C_ONES + P]
        iota = cst[:, C_IOTA:C_IOTA + P]
        X = sb("X", [P, NT, D])
        fc_sb = sb("fc_sb", [P, DC, 2 * D])
        fcb_sb = sb("fcb_sb", [1, D])
        wb_sb = sb("wb_sb", [P, DC, D])
        wr_sb = sb("wr_sb", [P, DC, E])
        br_sb = sb("br_sb", [P, E])
        rs0 = sb("rs0", [P, NT])
        nb0 = sb("nb0", [P, NT])
        eps = sb("eps", [P, 1])
        keyA = sb("keyA", [P, SORT_F])
        keyB = sb("keyB", [P, SORT_F])
        key_ext = sb("key_ext", [P, 2])
        idx = sb("idx", [P, W], I32)
        same = sb("same", [P, W])
        lo = sb("lo", [P, W], BF16)
        hi = sb("hi", [P, W], BF16)
        iota_b = sb("iota_b", [P, P], BF16)
        cnt = sb("cnt", [P, NT])
        hrow = sb("hrow", [P, NT], I32)
        psel = sb("psel", [P, NT])
        carry = sb("carry", [P, D])
        run = sb("run", [P, E])
        ftab = sb("ftab", [1, 2, FTILES], I32)
        ctab = sb("ctab", [1, E], I32)
        small = sb("small", [P, 8, NT])
        w56 = sb("w56", [P, E, FTILES])

        POOL_WORDS = 22400
        pool = sb("pool", [P, POOL_WORDS])

        class Area:
            def __init__(self):
                self.at = 0

            def take(self, *shape, dt=F32):
                n = 1
                for s in shape:
                    n *= s
                words = n if dt in (F32, I32) else n // 2
                a = pool[:, self.at:self.at + words]
                self.at += words
                assert self.at <= POOL_WORDS, self.at
                if dt != F32:
                    a = a.bitcast(dt)
                if len(shape) > 1:
                    names = "abc"[:len(shape)]
                    a = a.rearrange(f"p ({' '.join(names)}) -> p {' '.join(names)}",
                                    **{k: s for k, s in zip(names, shape)})
                return a

        a0 = Area()
        xn0 = a0.take(G, D)
        xT0 = a0.take(G, DC, P)
        h0 = a0.take(G, D)
        st0 = a0.take(G, 6)
        mv0 = a0.take(G, 2)
        sd0 = a0.take(G)
        kv = a0.take(SORT_F, dt=I32)
        kd = a0.take(SRC_F, dt=I32)

        a1 = Area()
        ring = a1.take(HALF, D)
        state = [a1.take(HALF, D) for _ in range(2)]
        iblk = [a1.take(HALF, dt=I32) for _ in range(2)]
        fblk = [a1.take(HALF) for _ in range(2)]
        ohl = a1.take(HALF, P, dt=BF16)
        ohh = a1.take(HALF, 50, dt=BF16)[:, :, 0:NT]
        wld = a1.take(DC * H)
        wpk = a1.take(PACK)
        rowa = a1.take(P)
        rowc = a1.take(P)
        diag = a1.take(2, P)
        bT = a1.take(2, P)
        cT = a1.take(2, P)

        a2 = Area()
        end = a2.take(G, D)
        nidx = a2.take(G, dt=I32)
        oht = a2.take(G, P)
        ohs = a2.take(G, P)
        agg = a2.take(G, D)
        aggT = a2.take(G, D)
        xin = a2.take(G, D)
        xinT = a2.take(G, D)
        rows = [a2.take(G, ROW) for _ in range(2)]
        st2 = a2.take(G, 6)
        mv2 = a2.take(G, 2)
        sd2 = a2.take(G)
        rs2 = a2.take(G)
        nb2 = a2.take(G)
        st3 = a2.take(G, 6)
        mv3 = a2.take(G, 2)
        sd3 = a2.take(G)
        rs3 = a2.take(G)
        nb3 = a2.take(G)
        lg = a2.take(G, E)
        rt = [a2.take(G, E) for _ in range(6)]
        rv = [a2.take(G) for _ in range(6)]
        pos_f = a2.take(2, G)
        pos_i = a2.take(2, G, dt=I32)
        mk = a2.take(G, E)
        rbase = a2.take(G, E)
        padrow = a2.take(2, ROW)
        zrow = a2.take(D)

        a3 = Area()
        spare = X[:, :, :].rearrange("p n d -> p (n d)")
        pk = [a3.take(PACK) for _ in range(2)] + [spare[:, i * PACK:(i + 1) * PACK] for i in range(XB - 2)]
        xs = [a3.take(SUB, ROW) for _ in range(XB)]
        xe = a3.take(DC, FT)
        xeh = a3.take(DC, FT, dt=F16)
        xel = a3.take(DC, FT, dt=F16)
        hf = a3.take(HC, FT)
        hh = a3.take(HC, FT, dt=F16)
        hl = a3.take(HC, FT, dt=F16)
        yt = a3.take(SUB, D)
        yw = a3.take(SUB, D)

        def halves(pack):
            v = pack[:, 0:PK_W].bitcast(F16)
            n = DC * H
            w1h, w1l = (v[:, i * n:(i + 1) * n].rearrange("p (k h) -> p k h", k=DC) for i in (0, 1))
            w2h, w2l = (v[:, i * n:(i + 1) * n].rearrange("p (c d) -> p c d", c=HC) for i in (2, 3))
            return w1h, w1l, w2h, w2l

        s_x = sem("x_loaded")
        s_xt = sem("x_tail_loaded")
        s_zero = sem("x_tail_zeroed")
        s_w = sem("weights_loaded")
        s_cst = sem("constants_loaded")
        s_edge = sem("edges_loaded")
        s_kpad = sem("key_padded")
        s_eps = sem("eps_set")
        s_bn0 = sem("bn0")
        s_mv0 = sem("mv0")
        s_sd0 = sem("sd0")
        s_rs0 = sem("rs0")
        s_nb0 = sem("nb0")
        s_xn0 = sem("xn0")
        s_t0 = sem("t0")
        s_xT0 = sem("xT0")
        s_m0 = sem("m0")
        s_h0 = sem("h0")
        s_b0 = sem("base0")
        s_hst = sem("h_stored")
        s_sort = sem("sort_step")
        s_st = sem("sort_turned")
        s_sc = sem("sort_turned_copied")
        s_kout = sem("keys_stored")
        s_kin = sem("keys_dealt")
        s_edge_t = sem("edge_tables")
        s_blk = sem("blocks_ready")
        s_g = [sem(f"gathered{i}") for i in range(HALF)]
        s_state = sem("state_step")
        s_hist = [sem(f"history_stored{i}") for i in range(2)]
        s_ohl = sem("onehot_lo")
        s_ohh = sem("onehot_hi")
        s_cm = sem("counted")
        s_wl = sem("w_loaded")
        s_hi = sem("w_high")
        s_lo = sem("w_low")
        s_wst = sem("pack_stored")
        s_tab = sem("node_table")
        s_tabm = sem("node_table_mm")
        s_cr = sem("carry_step")
        s_crm = sem("carry_mm")
        s_nblk = sem("node_block")
        s_end = [sem(f"end_gathered{i}") for i in range(G)]
        s_zst = sem("zero_row_stored")
        s_oht = sem("oht")
        s_ohT = sem("oht_turned")
        s_ohs = sem("ohs")
        s_cm2 = sem("carry_picked")
        s_agg = sem("agg")
        s_aT = sem("agg_turned")
        s_aTc = sem("aggT")
        s_my = sem("graph_product")
        s_x2 = sem("x2")
        s_bn2 = sem("bn2")
        s_mv2 = sem("mv2")
        s_sd2 = sem("sd2")
        s_rs2 = sem("rs2")
        s_nb2 = sem("nb2")
        s_xin = sem("xin")
        s_bn3 = sem("bn3")
        s_mv3 = sem("mv3")
        s_sd3 = sem("sd3")
        s_rs3 = sem("rs3")
        s_nb3 = sem("nb3")
        s_xiT = sem("xin_turned")
        s_xiTc = sem("xinT")
        s_lg = sem("logits")
        s_route = sem("route_step")
        s_exp = sem("exp")
        s_rank = sem("ranks")
        s_row = sem("rows_ready")
        s_scat = sem("rows_scattered")
        s_acc0 = sem("acc_started")
        s_ftab = sem("expert_table")
        s_padr = sem("pad_row")
        s_padst = sem("pads_stored")
        s_pk = [sem(f"pack_loaded{i}") for i in range(XB)]
        s_xs = [sem(f"slots_loaded{i}") for i in range(XB)]
        s_fT = sem("f_turned")
        s_xe = sem("xe")
        s_xh = sem("xe_high")
        s_xl = sem("xe_low")
        s_g1 = sem("product1")
        s_gelu = sem("gelu")
        s_hh = sem("h_high")
        s_hl = sem("h_low")
        s_g2 = sem("product2")
        s_yt = sem("y")
        s_yw = sem("y_weighted")
        s_add = sem("y_added")
        s_out = sem("out_stored")
        s_pool_on = sem("pool_went_on")
        s_v_on = sem("vector_went_on")

        keys = [keyA, keyB]
        h_tiles = h_dram.rearrange("(n p) d -> p n d", p=P)
        acc_tiles = acc.rearrange("(n p) d -> p n d", p=P)
        hist_cols = hist[0:ZERO_ROW, :].rearrange("(f p) d -> p f d", p=P)
        w1_v = w1.rearrange("e (k p) h -> e p k h", p=P)
        w2_v = w2.rearrange("e (c p) d -> e p c d", p=P)

        def pick(pe, at, t):
            pe.wait_ge(s_ohs, 1 + at + (t + 1))
            pe.wait_ge(s_agg, 1 + at + max(t - 1, 0))
            pe.matmul(bank[2 + t % 2][:, 0:D], ohs[:, t, :], carry[:, :], start=True, stop=True).then_inc(s_cm2, 1)

        def graph(pe, at, t):
            pe.wait_ge(s_aTc, 1 + at + (t + 1))
            pe.wait_ge(s_x2, 1 + at + max(t - 1, 0))
            for c in range(DC):
                mm = pe.matmul(bank[6 + t % 2][:, 0:D], aggT[:, t, c * P:(c + 1) * P], wb_sb[:, c, :],
                               start=c == 0, stop=c == DC - 1)
            mm.then_inc(s_my, 1)

        def logits(pe, k, at, t):
            pe.wait_ge(s_xiTc, 1 + at + (t + 1))
            if t == 0:
                pe.wait_ge(s_agg, 1 + at + G)
            for c in range(DC):
                mm = pe.matmul(bank[2][:, t * E:(t + 1) * E], xinT[:, t, c * P:(c + 1) * P], wr_sb[:, c, :],
                               start=c == 0, stop=c == DC - 1)
            mm.then_inc(s_lg, 1)

        def stats(v, a, s_in, st, s_bn, at, t):
            v.wait_ge(s_in, 1 + at + (t + 1))
            v.sem_inc(s_v_on, 1)
            v.bn_stats(st[:, t, :], a).then_inc(s_bn, 1)

        def aggregate(v, st, mv, s_bn, s_mv, at):
            for t in range(G):
                v.wait_ge(s_bn, at + (t + 1))
                v.sem_inc(s_v_on, 1)
                v.bn_aggr(mv[:, t, :], st[:, t, :]).then_inc(s_mv, 1)

        def route(v, k, at, first):
            n = [0]

            def st(ins):
                n[0] += 1
                ins.then_inc(s_route, 1)
                v.wait_ge(s_route, 1 + k * ROUTE_STEPS + n[0])

            def wide(a):
                return a.unsqueeze(2).to_broadcast([P, G, E])

            one1, one2, tmp, tmp2 = rt[0], rt[1], rt[2], rt[3]
            top1, top2, i1, diff, ex, den = rv
            iota_e = cst[:, C_EXP:C_EXP + G * E].rearrange("p (g e) -> p g e", g=G)
            v.wait_ge(s_lg, at + G)
            if not first:
                v.wait_ge(s_scat, 16 * 2 * G * k)
            st(v.tensor_tensor(lg, bank[2][:, 0:G * E].rearrange("p (g e) -> p g e", g=G),
                               br_sb[:, :].unsqueeze(1).to_broadcast([P, G, E]), ALU.add))

            def best(scores, top, onehot):
                st(v.tensor_reduce(top, scores, AX.X, ALU.max))
                st(v.tensor_tensor(tmp, scores, wide(top), ALU.is_lt))
                st(v.scalar_tensor_tensor(out=tmp, in0=tmp, scalar=float(E), in1=iota_e, op0=ALU.mult, op1=ALU.add))
                st(v.tensor_reduce(i1, tmp, AX.X, ALU.min))
                st(v.tensor_tensor(onehot, iota_e, wide(i1), ALU.is_equal))

            best(lg, top1, one1)
            st(v.scalar_tensor_tensor(out=tmp2, in0=one1, scalar=-3.0e38, in1=lg, op0=ALU.mult, op1=ALU.add))
            best(tmp2, top2, one2)
            st(v.tensor_tensor(mk, one1, one2, ALU.add))
            st(v.tensor_tensor(mk, mk, wide(cst[:, bass.ds(at + C_VALID, G)]), ALU.mult))
            assert n[0] == RANK_AT
            st(v.tensor_tensor(diff, top2, top1, ALU.subtract))
            assert n[0] == EXP_AT
            v.wait_ge(s_exp, k + 1)
            st(v.tensor_scalar(den, ex, 1.0, None, ALU.add))
            st(v.reciprocal(den, den))
            st(v.tensor_copy(rows[0][:, :, D + 1], den))
            st(v.tensor_tensor(rows[1][:, :, D + 1], ex, den, ALU.mult))
            for r in range(2):
                st(v.tensor_scalar(rows[r][:, :, D].bitcast(I32), cst[:, bass.ds(at + C_TOKEN, G)], 0.0, None, ALU.add))
            v.wait_ge(s_rank, k + 1)
            for t in range(G):
                src_ = run[:, :] if t == 0 else rbase[:, t - 1, :]
                if t == 0:
                    st(v.tensor_copy(rbase[:, 0, :], run[:, :]))
                else:
                    st(v.tensor_tensor(rbase[:, t, :], rbase[:, t - 1, :], bank[3][:, 64 + (t - 1) * E:64 + t * E],
                                       ALU.add))
            st(v.tensor_tensor(run[:, :], rbase[:, G - 1, :], bank[3][:, 64 + (G - 1) * E:64 + G * E], ALU.add))
            st(v.tensor_tensor(rbase, rbase, bank[3][:, 0:G * E].rearrange("p (g e) -> p g e", g=G), ALU.add))
            st(v.tensor_tensor(rbase, rbase, cst[:, C_EBASE:C_EBASE + G * E].rearrange("p (g e) -> p g e", g=G),
                               ALU.add))
            for r, one in enumerate((one1, one2)):
                st(v.tensor_tensor(tmp, one, rbase, ALU.mult))
                st(v.tensor_reduce(pos_f[:, r, :], tmp, AX.X, ALU.add))
                st(v.tensor_tensor(pos_f[:, r, :], pos_f[:, r, :], cst[:, bass.ds(at + C_VALID, G)], ALU.mult))
                st(v.tensor_tensor(pos_i[:, r, :], pos_f[:, r, :],
                                   cst[:, bass.ds(at + (C_TRASH, C_TRASH2)[r], G)], ALU.add))
            assert n[0] == ROUTE_STEPS, n[0]

        from_one = {
            "act": [s_xT0, s_b0, s_sd0, s_ohs, s_aTc, s_xiTc, s_xe],
            "vector": [s_state, s_lo, s_agg, s_x2, s_xin, s_route, s_xl, s_yt],
            "pe": [s_cm],
        }

        block = ctx.enter_context(nc.Block())

        @block.sync
        def _(sp):
            sp.dma_start(cst[:, :], const).then_inc(s_cst, 16)
            sp.dma_start(keyA[0:SRC_P, 0:SRC_F].bitcast(I32),
                         src.rearrange("(p f) -> p f", p=SRC_P)).then_inc(s_edge, 16)
            sp.dma_start(kd[0:SRC_P, :], dst.rearrange("(p f) -> p f", p=SRC_P)).then_inc(s_edge, 16)
            full = (NT - 1) * P
            sp.dma_start(X[:, 0:NT - 1, :], x[0:full, :].rearrange("(n p) d -> p n d", p=P)).then_inc(s_x, 16)
            sp.wait_ge(s_zero, 1)
            sp.dma_start(X[0:TAIL, NT - 1, :], x[full:N_NODES, :]).then_inc(s_xt, 16)
            sp.dma_start(fc_sb[:, :, :], fc.rearrange("(k p) n -> p k n", p=P)).then_inc(s_w, 16)
            sp.dma_start(fcb_sb[:, :], fc_b).then_inc(s_w, 16)
            sp.dma_start(wb_sb[:, :, :], w_bot.rearrange("(k p) n -> p k n", p=P)).then_inc(s_w, 16)
            sp.dma_start(wr_sb[:, :, :], wr.rearrange("(k p) n -> p k n", p=P)).then_inc(s_w, 16)
            sp.dma_start(br_sb[:, :], br).then_inc(s_w, 16)
            with sp.Fori(0, NG) as k:
                sp.wait_ge(s_h0, G * k + G)
                sp.dma_start(h_tiles[:, bass.ds(k * G, G), :], h0).then_inc(s_hst, 16)
            sp.wait_ge(s_sort, SORT_DONE)
            sp.dma_start(key_dram.rearrange("(p f) -> p f", p=P), keys[SORT_ENDS_IN][:, :]).then_inc(s_kout, 16)
            sp.wait_ge(s_kout, 16)
            sp.dma_start(keyB[:, 0:W], key_dram[0:W * P].rearrange("(p f) -> p f", p=P)).then_inc(s_kin, 16)
            before = key_dram[0:W * (P - 1)].rearrange("(p f) -> p f", f=W)
            with nc.allow_non_contiguous_dma(reason="one key of each partition"):
                sp.dma_start(key_ext[1:P, 0:1], before[:, W - 1:W]).then_inc(s_kin, 16)
                sp.dma_start(key_ext[1:P, 1:2], before[:, 0:1]).then_inc(s_kin, 16)

            def store_history(k, half):
                sp.wait_ge(s_state, 1 + 2 * HALF * k + HALF * (half + 1))
                sp.dma_start(hist_cols[:, bass.ds(2 * HALF * k + HALF * half, HALF), :],
                             state[half]).then_inc(s_hist[half], 16)

            def load_weights(k, part):
                w = w1_v if part == 0 else w2_v
                a = wld.rearrange("p (k h) -> p k h", k=DC if part == 0 else HC)
                sp.wait_ge(s_lo, 1 + 2 * k + part)
                sp.dma_start(a, w[bass.ds(k, 1)].rearrange("e p k h -> p (e k) h")).then_inc(s_wl, 16)

            sp.wait_ge(s_hst, 16 * NG)

            def prepare(k, first=False):
                for part in range(2):
                    t = 2 * k + part
                    load_weights(k, part)
                    if part == 0:
                        if not first:
                            sp.wait_ge(s_wst, 16 * k)
                        sp.dma_start(wpk[:, PK_W:PACK],
                                     params[bass.ds(k, 1)].rearrange("e p n -> p (e n)")).then_inc(s_wl, 16)
                    store_history(t, 0)
                    if part == 1:
                        sp.wait_ge(s_lo, 1 + 2 * k + 2)
                        sp.dma_start(packs[bass.ds(k, 1)].rearrange("e p n -> p (e n)"), wpk).then_inc(s_wst, 16)
                    store_history(t, 1)

            prepare(0, first=True)
            with sp.Fori(1, E) as k:
                prepare(k)
            with sp.Fori(2 * E, GTURNS) as k:
                store_history(k, 0)
                store_history(k, 1)
            sp.wait_ge(s_padr, 5)
            sp.dma_start(hist[ZERO_ROW:ZERO_ROW + 1, :], zrow[0:1, :]).then_inc(s_zst, 16)
            sp.dma_start(acc[ACC_PAD:ACC_ROWS, :], zrow).then_inc(s_acc0, 16)
            with sp.Fori(0, NG) as k:
                sp.wait_ge(s_x2, 1 + G * k + G)
                sp.dma_start(acc_tiles[:, bass.ds(k * G, G), :], X[:, bass.ds(k * G, G), :]).then_inc(s_acc0, 16)
            sp.wait_ge(s_ftab, FTAB_STEPS)
            for e in range(E):
                c = sp.value_load(ctab[0:1, e:e + 1], min_val=0, max_val=(E - 1) * REGION + N_NODES)
                sp.dma_start(slots[bass.ds(c, FT), :].rearrange("(s p) r -> p s r", p=P), padrow).then_inc(s_padst, 16)
            sp.dma_start(slots[E * REGION:E * REGION + FT, :].rearrange("(s p) r -> p s r", p=P),
                         padrow).then_inc(s_padst, 16)
            sp.wait_ge(s_padst, 16 * (E + 1))
            sp.wait_ge(s_scat, 16 * 2 * NT)

            def load_slots(j, b):
                r = sp.value_load(ftab[0:1, 1, bass.ds(j, 1)], min_val=0, max_val=E * REGION)
                sp.dma_start(xs[b], slots[bass.ds(r, FT), :].rearrange("(s p) r -> p s r", p=P)).then_inc(s_xs[b], 16)

            def load_pack(j, b):
                e = sp.value_load(ftab[0:1, 0, bass.ds(j, 1)], min_val=0, max_val=E - 1)
                sp.dma_start(pk[b], packs[bass.ds(e, 1)].rearrange("e p n -> p (e n)")).then_inc(s_pk[b], 16)

            for b in range(2):
                load_slots(b, b)
                load_pack(b, b)
            sp.wait_ge(s_acc0, 16 * (NG + 1))
            for b in range(2, XB):
                load_slots(b, b)
                load_pack(b, b)
            with sp.Fori(0, FTILES // XB - 1) as t:
                for b in range(XB):
                    sp.wait_ge(s_yt, 1 + SUB * (t * XB + b) + SUB)
                    load_pack(t * XB + (b + XB), b)
                    sp.wait_ge(s_add, 16 * SUB * (t * XB + b) + 16 * SUB)
                    load_slots(t * XB + (b + XB), b)
            sp.wait_ge(s_add, 16 * SUB * FTILES)
            sp.dma_start(out, acc[0:N_NODES, :]).then_inc(s_out, 16)
            sp.wait_ge(s_out, 16)
            sp.wait_ge(s_hst, 16 * NG)
            sp.wait_ge(s_wst, 16 * E)
            sp.wait_ge(s_acc0, 16 * (NG + 1))

        @block.gpsimd
        def _(pool_e):
            h_bound = pool_e.to_reg(NT * P - 1)
            hist_bound = pool_e.to_reg(ZERO_ROW)
            slot_bound = pool_e.to_reg(SLOT_ROWS - 1)
            acc_bound = pool_e.to_reg(ACC_ROWS - 1)
            pool_e.wait_ge(s_hst, 16 * NG)

            def gather_half(k, half, first=False):
                pool_e.wait_ge(s_blk, 2 * k + (half + 1))
                pool_e.sem_inc(s_pool_on, 1)
                for u in range(HALF):
                    if not first:
                        pool_e.wait_ge(s_state, 1 + 2 * HALF * k + (HALF * (half - 1) + u + 1))
                        pool_e.sem_inc(s_pool_on, 1)
                    pool_e.indirect_dma_start(
                        ring[:, u, :], None, h_dram, bass.IndirectOffsetOnAxis(iblk[half][:, u:u + 1], 0),
                        bounds_check=h_bound, oob_is_err=True).then_inc(s_g[u], 16)

            gather_half(0, 0, first=True)
            gather_half(0, 1)
            with pool_e.Fori(1, GTURNS) as k:
                gather_half(k, 0)
                gather_half(k, 1)

            def gather_ends(k):
                pool_e.wait_ge(s_nblk, k + 1)
                pool_e.wait_ge(s_agg, 1 + k * G)
                pool_e.sem_inc(s_pool_on, 1)
                for t in range(G):
                    pool_e.indirect_dma_start(
                        end[:, t, :], None, hist, bass.IndirectOffsetOnAxis(nidx[:, t:t + 1], 0),
                        bounds_check=hist_bound, oob_is_err=True).then_inc(s_end[t], 16)

            def scatter_rows(k):
                pool_e.wait_ge(s_route, 1 + (k + 1) * ROUTE_STEPS)
                for t in range(G):
                    pool_e.wait_ge(s_row, (k * G + (t + 1)) * 2)
                    pool_e.sem_inc(s_pool_on, 1)
                    for r in range(2):
                        pool_e.indirect_dma_start(
                            slots, bass.IndirectOffsetOnAxis(pos_i[:, r, t:t + 1], 0), rows[r][:, t, :], None,
                            bounds_check=slot_bound, oob_is_err=True).then_inc(s_scat, 16)

            pool_e.wait_ge(s_hist[0], 16 * GTURNS)
            pool_e.wait_ge(s_hist[1], 16 * GTURNS)
            pool_e.wait_ge(s_zst, 16)
            gather_ends(0)
            with pool_e.Fori(0, NG - 1) as k:
                gather_ends(k + 1)
                scatter_rows(k)
            scatter_rows(NG - 1)

            pool_e.wait_ge(s_acc0, 16 * (NG + 1))

            def add_rows(t, first=False):
                for b in range(XB):
                    for s in range(SUB):
                        pool_e.wait_ge(s_yw, SUB * (t * XB + b) + (s + 1))
                        if not (first and b == 0 and s == 0):
                            pool_e.wait_ge(s_add, 16 * (SUB * (t * XB + b) + s))
                        pool_e.sem_inc(s_pool_on, 1)
                        pool_e.indirect_dma_start(
                            acc, bass.IndirectOffsetOnAxis(xs[b][:, s, D:D + 1].bitcast(I32), 0), yw[:, s, :], None,
                            bounds_check=acc_bound, oob_is_err=True, compute_op=ALU.add).then_inc(s_add, 16)

            add_rows(0, first=True)
            with pool_e.Fori(1, FTILES // XB) as t:
                add_rows(t)

        @block.scalar
        def _(act):
            for s in from_one["act"]:
                act.sem_inc(s, 1)
            def normalize0(k, t):
                n = k * G + t
                act.activation(xn0[:, t, :], X[:, bass.ds(n, 1), :].rearrange("p n d -> p (n d)"), ACT.Identity,
                               bias=nb0[:, bass.ds(n, 1)], scale=rs0[:, bass.ds(n, 1)]).then_inc(s_xn0, 1)

            def turned0(k, t):
                act.wait_ge(s_t0, k * G + (t + 1))
                act.copy(xT0[:, t, :, :].rearrange("p k q -> p (k q)"), bank[t % 2][:, 0:D]).then_inc(s_xT0, 1)

            def hidden(k, t):
                n = k * G + t
                act.wait_ge(s_m0, k * G + (t + 1))
                if t == 0 and not (isinstance(k, int) and k == 0):
                    act.wait_ge(s_hst, 16 * k)
                act.activation(h0[:, t, :], bank[2 + t % 3][:, 0:D], ACT.Relu).then_inc(s_h0, 1)
                act.activation(X[:, bass.ds(n, 1), :].rearrange("p n d -> p (n d)"), bank[2 + t % 3][:, D:2 * D],
                               ACT.Copy).then_inc(s_b0, 1)

            def tiles0(tiles):
                for k, t in tiles:
                    normalize0(k, t)
                for i, (k, t) in enumerate(tiles):
                    turned0(k, t)
                    if i >= 1:
                        hidden(*tiles[i - 1])
                hidden(*tiles[-1])

            with act.Fori(0, NG) as k:
                act.wait_ge(s_mv0, k * G + G)
                act.wait_ge(s_eps, 1)
                act.activation(sd0, mv0[:, :, 1], ACT.Sqrt, bias=eps[:, 0:1]).then_inc(s_sd0, 1)
            act.wait_ge(s_nb0, NG)
            tiles0([(0, t) for t in range(G)])
            with act.Fori(1, EARLY) as k:
                tiles0([(k, t) for t in range(G)])
            for m in range(2 * (LEVELS - FREE_LEVELS)):
                to = keys[1 - SORT_TURN_FROM[m]]
                for q in range(2):
                    act.wait_ge(s_st, 2 * m + q + 1)
                    act.copy(to[:, q * 512:(q + 1) * 512], bank[5 + q][:, :]).then_inc(s_sc, 1)
                if m % 2 == 1:
                    tiles0(LATE_TILES[m // 2])

            def blocks(k, half, first=False):
                if not first:
                    act.wait_ge(s_state, 1 + 2 * HALF * k + HALF * (half - 1))
                at = 2 * HALF * k + HALF * half
                act.copy(fblk[half], same[:, bass.ds(at, HALF)])
                act.copy(iblk[half], idx[:, bass.ds(at, HALF)]).then_inc(s_blk, 1)

            def high(k, part):
                w1h, w1l, w2h, w2l = halves(wpk)
                dst_ = w1h if part == 0 else w2h
                a = wld.rearrange("p (k h) -> p k h", k=DC if part == 0 else HC)
                act.wait_ge(s_wl, 48 * k + (32 if part == 0 else 48))
                act.activation(dst_, a, ACT.Copy, scale=WS).then_inc(s_hi, 1)

            act.wait_ge(s_edge_t, EDGE_STEPS)
            blocks(0, 0, first=True)
            blocks(0, 1, first=True)
            high(0, 0)
            blocks(1, 0)
            blocks(1, 1)
            high(0, 1)
            with act.Fori(1, E) as k:
                for part in range(2):
                    blocks(2 * k + part, 0)
                    blocks(2 * k + part, 1)
                    high(k, part)
            with act.Fori(2 * E, GTURNS) as k:
                blocks(k, 0)
                blocks(k, 1)
            act.wait_ge(s_crm, 2)
            act.copy(carry[:, :], bank[7][:, 0:D]).then_inc(s_cr, 1)

            act.wait_ge(s_tab, TAB_STEPS)
            act.copy(nidx, hrow[:, 0:G]).then_inc(s_nblk, 1)

            def nodes(k, first=False, last=False):
                for t in range(G):
                    act.wait_ge(s_ohT, k * G + (t + 1))
                    act.copy(ohs[:, t, :], bank[t % 2][:, 0:P]).then_inc(s_ohs, 1)
                for t in range(G):
                    act.wait_ge(s_aT, k * G + (t + 1))
                    act.copy(aggT[:, t, :], bank[4 + t % 2][:, 0:D]).then_inc(s_aTc, 1)
                if not last:
                    act.wait_ge(s_agg, 1 + k * G + G)
                    act.copy(nidx, hrow[:, bass.ds(k * G + G, G)]).then_inc(s_nblk, 1)
                act.wait_ge(s_mv2, k * G + G)
                act.activation(sd2, mv2[:, :, 1], ACT.Sqrt, bias=eps[:, 0:1]).then_inc(s_sd2, 1)
                for t in range(G):
                    act.wait_ge(s_xiT, k * G + (t + 1))
                    act.copy(xinT[:, t, :], bank[t % 2][:, 0:D]).then_inc(s_xiTc, 1)
                act.wait_ge(s_mv3, k * G + G)
                act.activation(sd3, mv3[:, :, 1], ACT.Sqrt, bias=eps[:, 0:1]).then_inc(s_sd3, 1)
                act.wait_ge(s_nb3, k + 1)
                if not first:
                    act.wait_ge(s_scat, 16 * 2 * G * k)
                for t in range(G):
                    for r in range(2):
                        act.activation(rows[r][:, t, 0:D], xin[:, t, :], ACT.Identity, bias=nb3[:, t:t + 1],
                                       scale=rs3[:, t:t + 1]).then_inc(s_row, 1)
                act.wait_ge(s_route, 1 + k * ROUTE_STEPS + EXP_AT)
                act.activation(rv[4], rv[3], ACT.Exp).then_inc(s_exp, 1)

            nodes(0, first=True)
            with act.Fori(1, NG - 1) as k:
                nodes(k)
            nodes(NG - 1, last=True)

            def inputs(k, b, nxt=0):
                j = k * XB + b
                act.wait_ge(s_pk[b], 16 * k + 16)
                act.wait_ge(s_fT, j + 1)
                act.wait_ge(s_xl, 1 + j)
                for c in range(DC):
                    act.activation(xe[:, c, :], bank[0][:, c * FT:(c + 1) * FT], ACT.Identity,
                                   bias=pk[b][:, PK_B + c:PK_B + c + 1],
                                   scale=pk[b][:, PK_G + c:PK_G + c + 1]).then_inc(s_xe, 1)

            def gelus(k, b):
                j = k * XB + b
                for c in range(HC):
                    act.wait_ge(s_g1, HC * j + (2 * (c // 2) + 2))
                    act.activation(hf[:, c, :], bank[1 + c // 2][:, (c % 2) * FT:(c % 2 + 1) * FT], ACT.Gelu,
                                   bias=pk[b][:, PK_B1 + c:PK_B1 + c + 1], scale=1.0 / WS).then_inc(s_gelu, 1)

            inputs(0, 0)
            with act.Fori(0, FTILES // XB - 1) as k:
                for b in range(XB):
                    gelus(k, b)
                    inputs(k + (b + 1) // XB, (b + 1) % XB)
            for b in range(XB):
                gelus(FTILES // XB - 1, b)
                if b + 1 < XB:
                    inputs(FTILES // XB - 1, b + 1)

        @block.tensor
        def _(pe):
            for s in from_one["pe"]:
                pe.sem_inc(s, 1)
            pe.wait_ge(s_w, 16 * 5)
            pe.wait_ge(s_cst, 16)

            def turn0(k, t):
                pe.wait_ge(s_xn0, k * G + (t + 1))
                pe.wait_ge(s_xT0, 1 + k * G + max(t - 1, 0))
                for c in range(DC):
                    mm = pe.transpose(bank[t % 2][:, c * P:(c + 1) * P], xn0[:, t, c * P:(c + 1) * P], ident)
                mm.then_inc(s_t0, 1)

            def product0(k, t):
                pe.wait_ge(s_xT0, 1 + k * G + (t + 1))
                pe.wait_ge(s_b0, 1 + k * G + max(t - 2, 0))
                b = bank[2 + t % 3]
                n = k * G + t
                for c in range(DC):
                    pe.matmul(b[:, :], xT0[:, t, c, :], fc_sb[:, c, :], start=c == 0, stop=False)
                pe.matmul(b[:, 0:D], ones[0:1, :], fcb_sb[:, :], start=False, stop=False)
                pe.matmul(b[:, D:2 * D], ident, X[:, bass.ds(n, 1), :].rearrange("p n d -> p (n d)"),
                          start=False, stop=True).then_inc(s_m0, 1)

            def tiles0(tiles):
                for i, (k, t) in enumerate(tiles):
                    turn0(k, t)
                    if i >= 1:
                        product0(*tiles[i - 1])
                product0(*tiles[-1])

            with pe.Fori(0, EARLY) as k:
                tiles0([(k, t) for t in range(G)])

            for m in range(2 * (LEVELS - FREE_LEVELS)):
                pe.wait_ge(s_sort, SORT_TURN_AT[m])
                fr = keys[SORT_TURN_FROM[m]]
                for q in range(2):
                    if m > 0:
                        pe.wait_ge(s_sc, 2 * m - 1 + q)
                    for c in range(4):
                        cc = 4 * q + c
                        mm = pe.transpose(bank[5 + q][:, c * P:(c + 1) * P], fr[:, cc * P:(cc + 1) * P], ident)
                    mm.then_inc(s_st, 1)
                if m % 2 == 1:
                    tiles0(LATE_TILES[m // 2])

            def count(k, half, first=False, last=False):
                pe.wait_ge(s_ohh, 2 * k + (half + 1))
                for u in range(HALF):
                    mm = pe.matmul(bank[7][:, 0:NT], ohl[:, u, :], ohh[:, u, :],
                                   start=first and u == 0, stop=last and u == HALF - 1)
                mm.then_inc(s_cm, 1)

            count(0, 0, first=True)
            count(0, 1)
            with pe.Fori(1, GTURNS - 1) as k:
                count(k, 0)
                count(k, 1)
            count(GTURNS - 1, 0)
            count(GTURNS - 1, 1, last=True)

            pe.wait_ge(s_tab, 1)
            pe.matmul(bank[6][:, 0:NT], tri, cnt[:, :], start=True, stop=True)
            pe.matmul(bank[6][:, 64:64 + NT], ones, cnt[:, :], start=True, stop=True).then_inc(s_tabm, 1)
            pe.wait_ge(s_state, 1 + 2 * HALF * GTURNS)
            pe.wait_ge(s_cr, CR_DIAG)
            for c in range(DC):
                pe.transpose(bank[4][:, c * P:(c + 1) * P], state[1][:, HALF - 1, c * P:(c + 1) * P], ident)
            for c in range(2):
                mm = pe.matmul(bank[5][:, c * P:(c + 1) * P], ones, diag[:, c, :], start=True, stop=True)
            mm.then_inc(s_crm, 1)
            pe.wait_ge(s_cr, CR_DONE)
            for c in range(DC):
                mm = pe.transpose(bank[7][:, c * P:(c + 1) * P], cT[:, c, :], ident)
            mm.then_inc(s_crm, 1)
            pe.wait_ge(s_cr, CR_DONE + 1)
            pe.wait_ge(s_tab, TAB_STEPS)

            with pe.Fori(0, NG) as k:
                at = k * G
                pe.wait_ge(s_xiTc, 1 + at)
                pe.wait_ge(s_route, 1 + k * ROUTE_STEPS)
                for t in range(G):
                    pe.wait_ge(s_oht, at + (t + 1))
                    pe.wait_ge(s_ohs, 1 + at + max(t - 1, 0))
                    pe.transpose(bank[t % 2][:, 0:P], oht[:, t, :], ident).then_inc(s_ohT, 1)
                    if t >= 1:
                        pick(pe, at, t - 1)
                pick(pe, at, G - 1)
                for t in range(G):
                    pe.wait_ge(s_agg, 1 + at + (t + 1))
                    pe.wait_ge(s_aTc, 1 + at + max(t - 1, 0))
                    for c in range(DC):
                        mm = pe.transpose(bank[4 + t % 2][:, c * P:(c + 1) * P], agg[:, t, c * P:(c + 1) * P], ident)
                    mm.then_inc(s_aT, 1)
                    if t >= 1:
                        graph(pe, at, t - 1)
                graph(pe, at, G - 1)
                for t in range(G):
                    pe.wait_ge(s_xin, 1 + at + (t + 1))
                    if t < 2:
                        pe.wait_ge(s_ohs, 1 + at + G)
                    pe.wait_ge(s_xiTc, 1 + at + max(t - 1, 0))
                    for c in range(DC):
                        mm = pe.transpose(bank[t % 2][:, c * P:(c + 1) * P], xin[:, t, c * P:(c + 1) * P], ident)
                    mm.then_inc(s_xiT, 1)
                    if t >= 1:
                        logits(pe, k, at, t - 1)
                logits(pe, k, at, G - 1)
                pe.wait_ge(s_route, 1 + k * ROUTE_STEPS + RANK_AT)
                pe.matmul(bank[3][:, 0:G * E], tri, mk.rearrange("p g e -> p (g e)"), start=True, stop=True)
                pe.matmul(bank[3][:, 64:64 + G * E], ones, mk.rearrange("p g e -> p (g e)"),
                          start=True, stop=True).then_inc(s_rank, 1)

            def turn(k, b):
                j = k * XB + b
                pe.wait_ge(s_xs[b], 16 * k + 16)
                pe.wait_ge(s_xe, 1 + DC * j)
                for c in range(DC):
                    for s in range(SUB):
                        mm = pe.transpose(bank[0][:, c * FT + s * P:c * FT + (s + 1) * P],
                                          xs[b][:, s, c * P:(c + 1) * P], ident)
                mm.then_inc(s_fT, 1)

            def product1(k, b):
                j = k * XB + b
                w1h, w1l, _, _ = halves(pk[b])
                pe.wait_ge(s_xl, 1 + j + 1)
                pe.wait_ge(s_pk[b], 16 * k + 16)
                for h in range(HC):
                    o = bank[1 + h // 2][:, (h % 2) * FT:(h % 2 + 1) * FT]
                    n = 0
                    for c in range(DC):
                        for w, a in ((w1h, xeh), (w1h, xel), (w1l, xeh)):
                            mm = pe.matmul(o, w[:, c, h * P:(h + 1) * P], a[:, c, :],
                                           start=n == 0, stop=n == 3 * DC - 1)
                            n += 1
                    mm.then_inc(s_g1, 1)

            def product2(k, b):
                j = k * XB + b
                _, _, w2h, w2l = halves(pk[b])
                pe.wait_ge(s_yt, 1 + SUB * j)
                for h in range(HC):
                    if h % 2 == 0:
                        pe.wait_ge(s_hl, (HC // 2) * j + (h // 2 + 1))
                    for s in range(SUB):
                        for i, (a, w) in enumerate(((hh, w2h), (hh, w2l), (hl, w2h))):
                            mm = pe.matmul(bank[5 + s][:, 0:D], a[:, h, s * P:(s + 1) * P], w[:, h, :],
                                           start=h == 0 and i == 0, stop=h == HC - 1 and i == 2)
                        if h == HC - 1:
                            mm.then_inc(s_g2, 1)

            turn(0, 0)
            with pe.Fori(0, FTILES // XB - 1) as k:
                for b in range(XB):
                    product1(k, b)
                    turn(k + (b + 1) // XB, (b + 1) % XB)
                    product2(k, b)
            for b in range(XB):
                product1(FTILES // XB - 1, b)
                if b + 1 < XB:
                    turn(FTILES // XB - 1, b + 1)
                product2(FTILES // XB - 1, b)

        @block.vector
        def _(v):
            for s in from_one["vector"]:
                v.sem_inc(s, 1)
            v.memset(X[:, NT - 1, :], 0.0).then_inc(s_zero, 1)
            v.memset(eps[:, :], EPS).then_inc(s_eps, 1)
            v.memset(kv.bitcast(F32), 512.0).then_inc(s_kpad, 1)
            v.memset(key_ext[:, :], 512.0).then_inc(s_kpad, 1)
            v.wait_ge(s_x, 16)
            v.wait_ge(s_xt, 16)
            v.wait_ge(s_cst, 16)
            v.wait_ge(s_w, 16 * 5)
            with v.Fori(0, NG) as k:
                for t in range(G):
                    v.bn_stats(st0[:, t, :], X[:, bass.ds(k * G + t, 1), :].rearrange("p n d -> p (n d)")
                               ).then_inc(s_bn0, 1)
                v.wait_ge(s_sd0, 1 + k)
                v.sem_inc(s_v_on, 1)
                for t in range(G):
                    v.wait_ge(s_bn0, k * G + (t + 1))
                    v.sem_inc(s_v_on, 1)
                    v.bn_aggr(mv0[:, t, :], st0[:, t, :]).then_inc(s_mv0, 1)
                v.wait_ge(s_sd0, 1 + k + 1)
                v.reciprocal(rs0[:, bass.ds(k * G, G)], sd0).then_inc(s_rs0, 1)
                v.wait_ge(s_rs0, k + 1)
                v.scalar_tensor_tensor(out=nb0[:, bass.ds(k * G, G)], in0=mv0[:, :, 0], scalar=-1.0,
                                       in1=rs0[:, bass.ds(k * G, G)], op0=ALU.mult, op1=ALU.mult).then_inc(s_nb0, 1)

            n = [0]

            def step(ins, wait=True):
                n[0] += 1
                ins.then_inc(s_sort, 1)
                if wait:
                    v.wait_ge(s_sort, n[0])

            v.wait_ge(s_edge, 32)
            v.wait_ge(s_kpad, 2)
            ks = keyA[0:SRC_P, 0:SRC_F].bitcast(I32)
            kb = keyB[0:SRC_P, 0:SRC_F].bitcast(I32)
            step(v.tensor_scalar(kb, ks, DST_BITS, None, ALU.logical_shift_left))
            step(v.tensor_tensor(ks, kb, kd[0:SRC_P, :], ALU.bitwise_or))
            step(v.tensor_scalar(kv[0:SRC_P, 0:SRC_F], ks, 1 << 30, None, ALU.bitwise_or))
            step(v.tensor_scalar(keyA[:, :], kv.bitcast(F32), cst[:, C_SIGN:C_SIGN + 1], None, ALU.mult))

            cur, nxt = keyA, keyB

            def split(a, j):
                return a[:, :].rearrange("p (n t j) -> p n t j", t=2, j=j)

            def exchange(j, mirror=False):
                nonlocal cur, nxt
                a, b = split(cur, j), split(nxt, j)
                if mirror:
                    low, high_r = a[:, :, 0, :], a[:, :, 1, ::-1]
                    high, low_r = a[:, :, 1, :], a[:, :, 0, ::-1]
                else:
                    low, high_r = a[:, :, 0, :], a[:, :, 1, :]
                    high, low_r = high_r, low
                step(v.tensor_tensor(b[:, :, 0, :], low, high_r, ALU.min), wait=False)
                step(v.tensor_tensor(b[:, :, 1, :], high, low_r, ALU.max))
                cur, nxt = nxt, cur

            for lv in range(1, FREE_LEVELS + 1):
                exchange(1 << (lv - 1), mirror=True)
                for d in reversed(range(lv - 1)):
                    exchange(1 << d)
            turns = 0
            for lv in range(FREE_LEVELS + 1, LEVELS + 1):
                j = C_SIGN + lv - FREE_LEVELS
                step(v.tensor_scalar(nxt[:, :], cur[:, :], cst[:, j:j + 1], None, ALU.mult))
                cur, nxt = nxt, cur
                assert n[0] == SORT_TURN_AT[turns] and cur is keys[SORT_TURN_FROM[turns]]
                v.wait_ge(s_sc, 2 * turns + 2)
                cur, nxt = nxt, cur
                assert cur is keys[1 - SORT_TURN_FROM[turns]]
                turns += 1
                for d in reversed(range(lv - FREE_LEVELS)):
                    exchange(1 << d)
                assert n[0] == SORT_TURN_AT[turns] and cur is keys[SORT_TURN_FROM[turns]]
                v.wait_ge(s_sc, 2 * turns + 2)
                cur, nxt = nxt, cur
                assert cur is keys[1 - SORT_TURN_FROM[turns]]
                turns += 1
                for d in reversed(range(FREE_LEVELS)):
                    exchange(1 << d)
            assert cur is keys[SORT_ENDS_IN]
            assert n[0] == SORT_DONE, n[0]

            m = [0]

            def tab(ins, wait=True):
                m[0] += 1
                ins.then_inc(s_edge_t, 1)
                if wait:
                    v.wait_ge(s_edge_t, m[0])

            v.wait_ge(s_kin, 48)
            v.wait_ge(s_hst, 16 * NG)
            kw = keyB[:, 0:W].bitcast(I32)
            sk = keyA[:, 0:W].bitcast(I32)
            ext = small[:, 0, 0:2].bitcast(I32)
            SRC_MASK = (1 << 14) - 1
            tab(v.tensor_scalar(idx[:, :], kw, (1 << DST_BITS) - 1, None, ALU.bitwise_and), wait=False)
            tab(v.tensor_scalar(sk, kw, DST_BITS, SRC_MASK, ALU.logical_shift_right, ALU.bitwise_and), wait=False)
            tab(v.tensor_scalar(ext, key_ext[:, :].bitcast(I32), DST_BITS, SRC_MASK, ALU.logical_shift_right,
                                ALU.bitwise_and), wait=False)
            tab(v.memset(same[:, 0:1], 0.0), wait=False)
            tab(v.memset(state[1][:, HALF - 1, :], 0.0), wait=False)
            tab(v.tensor_copy(iota_b[:, :], iota))
            tab(v.tensor_tensor(same[:, 1:W], sk[:, 1:W], sk[:, 0:W - 1], ALU.is_equal), wait=False)
            tab(v.tensor_tensor(small[:, 1, 0:1], sk[:, 0:1], ext[:, 0:1], ALU.is_equal), wait=False)
            tab(v.tensor_tensor(small[:, 1, 1:2], ext[:, 1:2], ext[:, 0:1], ALU.is_equal), wait=False)
            tab(v.tensor_scalar(kw, sk, 127, None, ALU.bitwise_and))
            tab(v.tensor_copy(lo[:, :], kw))
            tab(v.tensor_scalar(kw, sk, 7, None, ALU.logical_shift_right))
            tab(v.tensor_copy(hi[:, :], kw))
            assert m[0] == EDGE_STEPS, m[0]

            def onehots(k, half):
                at = 2 * HALF * k + HALF * half
                v.wait_ge(s_cm, 1 + 2 * k + half)
                v.tensor_tensor(ohl, iota_b[:, :].unsqueeze(1).to_broadcast([P, HALF, P]),
                                lo[:, bass.ds(at, HALF)].unsqueeze(2).to_broadcast([P, HALF, P]), ALU.is_equal)
                v.tensor_tensor(ohh, iota_b[:, 0:NT].unsqueeze(1).to_broadcast([P, HALF, NT]),
                                hi[:, bass.ds(at, HALF)].unsqueeze(2).to_broadcast([P, HALF, NT]),
                                ALU.is_equal).then_inc(s_ohh, 1)

            def scan(k, half, first=False):
                for u in range(HALF):
                    if u == 0:
                        v.wait_ge(s_blk, 2 * k + half + 1)
                        if not first:
                            v.wait_ge(s_hist[half], 16 * k)
                    v.wait_ge(s_g[u], 32 * k + 16 * (half + 1))
                    v.wait_ge(s_state, 1 + 2 * HALF * k + (HALF * half + u))
                    prev = state[half][:, u - 1, :] if u else state[1 - half][:, HALF - 1, :]
                    v.scalar_tensor_tensor(out=state[half][:, u, :], in0=prev, scalar=fblk[half][:, u:u + 1],
                                           in1=ring[:, u, :], op0=ALU.mult, op1=ALU.max).then_inc(s_state, 1)

            def low(k, part):
                w1h, w1l, w2h, w2l = halves(wpk)
                hi_, lo_ = (w1h, w1l) if part == 0 else (w2h, w2l)
                a = wld.rearrange("p (k h) -> p k h", k=DC if part == 0 else HC)
                v.wait_ge(s_hi, 2 * k + part + 1)
                v.scalar_tensor_tensor(out=lo_, in0=a, scalar=WS, in1=hi_, op0=ALU.mult,
                                       op1=ALU.subtract).then_inc(s_lo, 1)

            def turns(k, first=False):
                for part in range(2):
                    t = 2 * k + part
                    onehots(t, 0)
                    scan(t, 0, first and part == 0)
                    low(k, part)
                    onehots(t, 1)
                    scan(t, 1, first and part == 0)

            turns(0, first=True)
            with v.Fori(1, E) as k:
                turns(k)
            with v.Fori(2 * E, GTURNS) as k:
                for half in range(2):
                    onehots(k, half)
                    scan(k, half)

            c = [0]

            def nt(ins, wait=True):
                c[0] += 1
                ins.then_inc(s_tab, 1)
                if wait:
                    v.wait_ge(s_tab, c[0])

            start, tot, endp, pe_, ps_, nz, fe = (small[:, i, :] for i in (2, 3, 4, 5, 6, 7, 0))
            v.wait_ge(s_cm, 1 + 2 * GTURNS)
            nt(v.tensor_copy(cnt[:, :], bank[7][:, 0:NT]))
            v.wait_ge(s_tabm, 1)
            nt(v.tensor_copy(fe, bank[6][:, 64:64 + NT]))
            nt(v.tensor_tensor_scan(tot, ones[:, 0:NT], fe, 0.0, ALU.mult, ALU.add))
            nt(v.tensor_tensor(tot, tot, fe, ALU.subtract))
            nt(v.tensor_tensor(start, bank[6][:, 0:NT], tot, ALU.add))
            nt(v.scalar_tensor_tensor(out=endp, in0=cnt[:, :], scalar=-1.0, in1=start, op0=ALU.add, op1=ALU.add),
               wait=False)
            nt(v.tensor_scalar(nz, cnt[:, :], 0.0, None, ALU.is_gt))
            ROUND = 12582912.0
            for o, i in ((pe_, endp), (ps_, start)):
                nt(v.tensor_scalar(o, i, 0.5, 1.0 / W, ALU.add, ALU.mult))
                nt(v.tensor_scalar(o, o, -0.5, ROUND, ALU.add, ALU.add))
                nt(v.tensor_scalar(o, o, ROUND, None, ALU.subtract))
            nt(v.scalar_tensor_tensor(out=fe, in0=pe_, scalar=-float(W), in1=endp, op0=ALU.mult, op1=ALU.add))
            nt(v.scalar_tensor_tensor(out=fe, in0=fe, scalar=float(P), in1=pe_, op0=ALU.mult, op1=ALU.add))
            nt(v.scalar_tensor_tensor(out=fe, in0=fe, scalar=-float(ZERO_ROW), in1=nz, op0=ALU.add, op1=ALU.mult))
            nt(v.tensor_scalar(hrow[:, :], fe, float(ZERO_ROW), None, ALU.add))
            nt(v.tensor_tensor(ps_, pe_, ps_, ALU.is_gt))
            nt(v.tensor_tensor(ps_, ps_, nz, ALU.mult))
            nt(v.scalar_tensor_tensor(out=fe, in0=pe_, scalar=1.0, in1=ps_, op0=ALU.add, op1=ALU.mult))
            nt(v.tensor_scalar(psel[:, :], fe, -1.0, None, ALU.add))
            assert c[0] == TAB_STEPS, c[0]

            r = [0]

            def cr(ins, wait=True):
                r[0] += 1
                ins.then_inc(s_cr, 1)
                if wait:
                    v.wait_ge(s_cr, r[0])

            cr(v.tensor_tensor(small[:, 1, 2:3], small[:, 1, 0:1], small[:, 1, 1:2], ALU.mult))
            cr(v.tensor_scalar(diag[:, 0, :], ident, small[:, 1, 2:3], None, ALU.mult), wait=False)
            cr(v.tensor_scalar(diag[:, 1, :], ident, small[:, 1, 0:1], None, ALU.mult), wait=False)
            assert r[0] == CR_DIAG
            v.wait_ge(s_crm, 1)
            cr(v.tensor_copy(rowa, bank[5][:, 0:P]), wait=False)
            cr(v.tensor_copy(rowc, bank[5][:, P:2 * P]), wait=False)
            cr(v.memset(bT[:, :, 0:1], 0.0))
            for q in range(DC):
                cr(v.tensor_tensor(bT[:, q, 1:P], bank[4][:, q * P:q * P + P - 1], rowc[:, 1:P], ALU.mult))
                cr(v.tensor_tensor_scan(cT[:, q, :], rowa, bT[:, q, :], 0.0, ALU.mult, ALU.max), wait=False)
            assert r[0] == CR_DONE, r[0]
            v.wait_ge(s_crm, 2)
            v.wait_ge(s_cr, CR_DONE + 1)

            v.wait_ge(s_hist[0], 16 * GTURNS)
            v.wait_ge(s_hist[1], 16 * GTURNS)
            v.wait_ge(s_wst, 16 * E)
            v.memset(zrow, 0.0).then_inc(s_padr, 1)
            v.memset(run[:, :], 0.0).then_inc(s_padr, 1)
            v.memset(padrow, 0.0).then_inc(s_padr, 1)
            v.wait_ge(s_padr, 3)
            for s in range(2):
                v.tensor_copy(padrow[:, s, D:D + 1].bitcast(I32), cst[:, C_PADID:C_PADID + 1]).then_inc(s_padr, 1)

            def nodes(k, first=False):
                at = k * G
                for t in range(G):
                    v.tensor_scalar(oht[:, t, :], iota, psel[:, bass.ds(at + t, 1)], None,
                                    ALU.is_equal).then_inc(s_oht, 1)
                for t in range(G):
                    v.wait_ge(s_end[t], 16 * k + 16)
                    v.wait_ge(s_cm2, at + (t + 1))
                    v.tensor_tensor(agg[:, t, :], end[:, t, :], bank[2 + t % 2][:, 0:D], ALU.max).then_inc(s_agg, 1)
                for t in range(G):
                    xt = X[:, bass.ds(at + t, 1), :].rearrange("p n d -> p (n d)")
                    v.wait_ge(s_my, at + (t + 1))
                    v.tensor_tensor(xt, xt, bank[6 + t % 2][:, 0:D], ALU.add).then_inc(s_x2, 1)
                    if t >= 1:
                        stats(v, X[:, bass.ds(at + t - 1, 1), :].rearrange("p n d -> p (n d)"),
                              s_x2, st2, s_bn2, at, t - 1)
                stats(v, X[:, bass.ds(at + G - 1, 1), :].rearrange("p n d -> p (n d)"), s_x2, st2, s_bn2, at, G - 1)
                aggregate(v, st2, mv2, s_bn2, s_mv2, at)
                v.wait_ge(s_sd2, k + 1)
                v.reciprocal(rs2, sd2).then_inc(s_rs2, 1)
                v.wait_ge(s_rs2, k + 1)
                for t in range(G):
                    v.tensor_scalar(xin[:, t, :], X[:, bass.ds(at + t, 1), :].rearrange("p n d -> p (n d)"),
                                    mv2[:, t, 0:1], rs2[:, t:t + 1], ALU.subtract, ALU.mult).then_inc(s_xin, 1)
                    if t >= 1:
                        stats(v, xin[:, t - 1, :], s_xin, st3, s_bn3, at, t - 1)
                stats(v, xin[:, G - 1, :], s_xin, st3, s_bn3, at, G - 1)
                aggregate(v, st3, mv3, s_bn3, s_mv3, at)
                v.wait_ge(s_sd3, k + 1)
                v.reciprocal(rs3, sd3).then_inc(s_rs3, 1)
                v.wait_ge(s_rs3, k + 1)
                v.scalar_tensor_tensor(out=nb3, in0=mv3[:, :, 0], scalar=-1.0, in1=rs3, op0=ALU.mult,
                                       op1=ALU.mult).then_inc(s_nb3, 1)
                route(v, k, at, first)

            nodes(0, first=True)
            with v.Fori(1, NG) as k:
                nodes(k)

            f = [0]

            def ft(ins):
                f[0] += 1
                ins.then_inc(s_ftab, 1)
                v.wait_ge(s_ftab, f[0])

            tiles, upto, ge = rv[0], rv[1], w56
            t8 = small[:, 0, 0:E]
            c8 = small[:, 1, 0:E]
            fx, fy = small[:, 2:4, :].rearrange("p a n -> p (a n)")[:, 0:FTILES], \
                small[:, 4:6, :].rearrange("p a n -> p (a n)")[:, 0:FTILES]
            ft(v.tensor_scalar(t8, run[:, :], FT - 0.5, 1.0 / FT, ALU.add, ALU.mult))
            ft(v.tensor_scalar(t8, t8, -0.5, ROUND, ALU.add, ALU.add))
            ft(v.tensor_scalar(t8, t8, ROUND, None, ALU.subtract))
            ft(v.tensor_tensor_scan(c8, ones[:, 0:E], t8, 0.0, ALU.mult, ALU.add))
            for e in range(E):
                ft(v.tensor_scalar(ge[:, e, :], cst[:, C_TILE:C_TILE + FTILES], c8[:, e:e + 1], None, ALU.is_ge))
            ft(v.tensor_reduce(fx, ge[:, :, :].rearrange("p e t -> p t e"), AX.X, ALU.add))
            for e in range(E):
                ft(v.tensor_scalar(ge[:, e, :], ge[:, e, :], t8[:, e:e + 1], None, ALU.mult))
            ft(v.tensor_reduce(fy, ge[:, :, :].rearrange("p e t -> p t e"), AX.X, ALU.add))
            ft(v.tensor_tensor(fy, cst[:, C_TILE:C_TILE + FTILES], fy, ALU.subtract))
            ft(v.tensor_scalar(fy, fy, float(FT), None, ALU.mult))
            ft(v.scalar_tensor_tensor(out=fy, in0=fx, scalar=float(REGION), in1=fy, op0=ALU.mult, op1=ALU.add))
            ft(v.tensor_scalar(ftab[:, 1, :], fy[0:1, :], float(E * REGION), None, ALU.min))
            ft(v.tensor_scalar(ftab[:, 0, :], fx[0:1, :], float(E - 1), None, ALU.min))
            ft(v.tensor_tensor(ctab[:, :], run[0:1, :], cst[0:1, C_EBASE:C_EBASE + E], ALU.add))
            assert f[0] == FTAB_STEPS, f[0]

            def split_inputs(k, b):
                j = k * XB + b
                v.wait_ge(s_xe, 1 + DC * j + DC)
                v.tensor_copy(xeh, xe).then_inc(s_xh, 1)
                v.wait_ge(s_xh, j + 1)
                v.tensor_tensor(xel, xe, xeh, ALU.subtract).then_inc(s_xl, 1)

            def split_hidden(k, b):
                j = k * XB + b
                for q in range(HC // 2):
                    a, hq, lq = (z[:, 2 * q:2 * q + 2, :] for z in (hf, hh, hl))
                    v.wait_ge(s_gelu, HC * j + (2 * q + 2))
                    v.tensor_copy(hq, a).then_inc(s_hh, 1)
                    v.wait_ge(s_hh, (HC // 2) * j + (q + 1))
                    v.tensor_tensor(lq, a, hq, ALU.subtract).then_inc(s_hl, 1)

            def results(k, b, first=False):
                j = k * XB + b
                for s in range(SUB):
                    v.wait_ge(s_g2, SUB * j + (s + 1))
                    v.scalar_tensor_tensor(out=yt[:, s, :], in0=bank[5 + s][:, 0:D], scalar=1.0 / WS,
                                           in1=pk[b][:, PK_B2:PK_B2 + D], op0=ALU.mult,
                                           op1=ALU.add).then_inc(s_yt, 1)
                if not first:
                    v.wait_ge(s_add, 16 * SUB * j)
                for s in range(SUB):
                    v.wait_ge(s_yt, 1 + SUB * j + (s + 1))
                    v.tensor_scalar(yw[:, s, :], yt[:, s, :], xs[b][:, s, D + 1:D + 2], None,
                                    ALU.mult).then_inc(s_yw, 1)

            split_inputs(0, 0)
            for b in range(XB):
                split_hidden(0, b)
                split_inputs((b + 1) // XB, (b + 1) % XB)
                results(0, b, first=b == 0)
            with v.Fori(1, FTILES // XB - 1) as k:
                for b in range(XB):
                    split_hidden(k, b)
                    split_inputs(k + (b + 1) // XB, (b + 1) % XB)
                    results(k, b)
            for b in range(XB):
                split_hidden(FTILES // XB - 1, b)
                if b + 1 < XB:
                    split_inputs(FTILES // XB - 1, b + 1)
                results(FTILES // XB - 1, b)


_INS = ["x", "src", "dst", "fc", "fc_b", "w_bot", "wr", "br", "params", "w1", "w2", "const"]


def lay_out(i):
    import numpy as np

    a = {k: np.asarray(v) for k, v in i.items()}
    wm = a["L0_gnn_weights_matrix"]
    params = np.concatenate([
        a["L0_ffn_ln_g"].reshape(E, DC, P).transpose(0, 2, 1),
        a["L0_ffn_ln_b"].reshape(E, DC, P).transpose(0, 2, 1),
        a["L0_ffn_b1"].reshape(E, HC, P).transpose(0, 2, 1),
        np.broadcast_to(a["L0_ffn_b2"][:, None, :], (E, P, D)),
    ], axis=2)
    return {
        "x": a["x"], "src": a["src"], "dst": a["dst"],
        "fc": np.concatenate([a["L0_gnn_fc_w"], wm[0:D]], axis=1),
        "fc_b": a["L0_gnn_fc_b"][None],
        "w_bot": np.ascontiguousarray(wm[D:2 * D]),
        "wr": a["L0_ffn_Wr"], "br": np.ascontiguousarray(np.broadcast_to(a["L0_ffn_br"], (P, E))),
        "params": np.ascontiguousarray(params),
        "w1": a["L0_ffn_W1"], "w2": a["L0_ffn_W2"],
        "const": constants(),
    }


def kernel(**inputs):
    import concourse.bacc as _bacc
    from concourse import mybir as _mybir
    from concourse.bass_utils import run_bass_kernel_spmd as _run

    laid = lay_out(inputs)
    nc = _bacc.Bacc("TRN2", target_bir_lowering=False, num_devices=1)
    args = [nc.dram_tensor(f"in_{n}", laid[n].shape, _mybir.dt.from_np(laid[n].dtype), kind="ExternalInput").ap()
            for n in _INS]
    args.append(nc.dram_tensor("out_x", (N_NODES, D), F32, kind="ExternalOutput").ap())
    gnn_moe_kernel(nc, *args)
    r = _run(nc, [{f"in_{n}": laid[n] for n in _INS}], core_ids=[0])
    return r.results[0]["out_x"]
```

```python
from contextlib import ExitStack

import concourse.bass as bass
from concourse import mybir

F32 = mybir.dt.float32
F16 = mybir.dt.float16
BF16 = mybir.dt.bfloat16
I32 = mybir.dt.int32
ALU = mybir.AluOpType
ACT = mybir.ActivationFunctionType
AX = mybir.AxisListType

P = 128
N_NODES = 6250
N_EDGES = 100000
D = 256
DC = D // P
E = 8
H = 1024
HC = H // P
EPS = 1e-5

NT = -(-N_NODES // P)
G = 7
NG = NT // G
TAIL = N_NODES - (NT - 1) * P

SORT_F = 1024
SRC_P, SRC_F = 125, 800
DST_BITS = 13
LEVELS = 17
FREE_LEVELS = 10
W = -(-N_EDGES // P)
HALF = 17
GTURNS = W // (2 * HALF)
ZERO_ROW = W * P

FT = 256
SUB = FT // P
REGION = 6528
EARLY = 2
FTILES = (2 * N_NODES + E * (FT - 1)) // FT
SLOT_ROWS = E * REGION + FT + 2 * P
TRASH = E * REGION + FT
ROW = D + 2
ACC_PAD = NT * P
ACC_ROWS = ACC_PAD + P
WS = 64.0
XB = 4

PK_W = 2 * (DC * H + HC * D) // 2
PK_G = PK_W
PK_B = PK_G + DC
PK_B1 = PK_B + DC
PK_B2 = PK_B1 + HC
PACK = PK_B2 + D

assert NG * G == NT and GTURNS * 2 * HALF == W and SRC_P * SRC_F == N_EDGES
assert FTILES % XB == 0 and 2 * E <= GTURNS

C_IDENT = 0
C_TRI = C_IDENT + P
C_ONES = C_TRI + P
C_IOTA = C_ONES + P
C_SIGN = C_IOTA + P
C_EXP = C_SIGN + LEVELS - FREE_LEVELS + 1
C_EBASE = C_EXP + G * E
C_VALID = C_EBASE + G * E
C_TRASH = C_VALID + NT
C_TRASH2 = C_TRASH + NT
C_TOKEN = C_TRASH2 + NT
C_TILE = C_TOKEN + NT
C_PADID = C_TILE + FTILES
C_ALL = C_PADID + 1


EDGE_STEPS = 13
TAB_STEPS = 24
CR_DIAG = 3
CR_DONE = 10
CR_SPLIT = 16
FTAB_STEPS = 29
RANK_AT = 14
EXP_AT = 15
PAD_STEPS = 4
RANKS_OUT = 16
ROUTE_STEPS = 35
SORT_TURN_AT = []
_n = 4 + FREE_LEVELS * (FREE_LEVELS + 1)
for _m in range(1, LEVELS - FREE_LEVELS + 1):
    SORT_TURN_AT += [_n + 1, _n + 1 + 2 * _m + 2]
    _n = SORT_TURN_AT[-1] + 2 * FREE_LEVELS
SORT_DONE = _n
_flips = FREE_LEVELS * (FREE_LEVELS + 1) // 2
SORT_TURN_FROM = []
for _m in range(1, LEVELS - FREE_LEVELS + 1):
    SORT_TURN_FROM += [(_flips + 1) % 2, (_flips + 1 + 1 + _m) % 2]
    _flips += 1 + 1 + _m + 1 + FREE_LEVELS
SORT_ENDS_IN = _flips % 2


_late = [divmod(_t, G) for _t in range(EARLY * G, NT)]
LATE_TILES = []
for _n in (0, 4, 0, 4, 1, 4, 1, 4, 1, 4, 2, 4, 3, 3):
    LATE_TILES.append(_late[:_n])
    _late = _late[_n:]
assert not _late and len(LATE_TILES) == 2 * (LEVELS - FREE_LEVELS)


def constants():
    import numpy as np

    c = np.zeros((P, C_ALL), np.float32)
    p = np.arange(P)
    c[:, C_IDENT:C_IDENT + P] = np.eye(P)
    c[:, C_TRI:C_TRI + P] = p[:, None] < p[None, :]
    c[:, C_ONES:C_ONES + P] = 1
    c[:, C_IOTA:C_IOTA + P] = p[None, :]
    sign = [1 - 2 * ((p >> (lv - FREE_LEVELS)) & 1) for lv in range(FREE_LEVELS, LEVELS + 1)]
    c[:, C_SIGN] = sign[0]
    for j in range(1, len(sign)):
        c[:, C_SIGN + j] = sign[j - 1] * sign[j]
    c[:, C_EXP:C_EXP + G * E] = np.tile(np.arange(E), G)
    c[:, C_EBASE:C_EBASE + G * E] = np.tile(np.arange(E) * REGION, G)
    node = np.arange(NT)[None, :] * P + p[:, None]
    c[:, C_VALID:C_VALID + NT] = node < N_NODES
    c[:, C_TRASH:C_TRASH + NT] = (node >= N_NODES) * (TRASH + p[:, None])
    c[:, C_TRASH2:C_TRASH2 + NT] = (node >= N_NODES) * (TRASH + P + p[:, None])
    c[:, C_TOKEN:C_TOKEN + NT] = node
    c[:, C_TILE:C_TILE + FTILES] = np.arange(FTILES)
    c[:, C_PADID] = ACC_PAD + p
    return c


def gnn_moe_kernel(nc, x, src, dst, fc, fc_b, w_bot, wr, br, params, w1, w2, const, out, scratch_kind="Internal"):
    ctx = ExitStack()
    with ctx:
        def sb(name, shape, dt=F32):
            return ctx.enter_context(nc.sbuf_tensor(name, shape, dt))

        def sem(name):
            return ctx.enter_context(nc.semaphore(name))

        def dram(name, shape, dt=F32):
            return nc.dram_tensor(name, shape, dt, kind=scratch_kind).ap()

        h_dram = dram("h_rows", [NT * P, D])
        key_dram = dram("sorted_keys", [P * SORT_F])
        hist = dram("history", [ZERO_ROW + 1, D])
        slots = dram("slots", [SLOT_ROWS, ROW])
        acc = out
        packs = dram("packs", [E, P, PACK])

        bank = [ctx.enter_context(nc.psum_tensor(f"bank{i}", [P, 512], F32)) for i in range(8)]

        cst = sb("cst", [P, C_ALL])
        ident = cst[:, C_IDENT:C_IDENT + P]
        tri = cst[:, C_TRI:C_TRI + P]
        ones = cst[:, C_ONES:C_ONES + P]
        iota = cst[:, C_IOTA:C_IOTA + P]
        X = sb("X", [P, NT, D])
        fc_sb = sb("fc_sb", [P, DC, 2 * D])
        fcb_sb = sb("fcb_sb", [1, D])
        wb_sb = sb("wb_sb", [P, DC, D])
        wr_sb = sb("wr_sb", [P, DC, E])
        br_sb = sb("br_sb", [P, E])
        rs0 = sb("rs0", [P, NT])
        nb0 = sb("nb0", [P, NT])
        eps = sb("eps", [P, 1])
        warm = sb("warm", [P, 1])
        keyA = sb("keyA", [P, SORT_F])
        keyB = sb("keyB", [P, SORT_F])
        key_ext = sb("key_ext", [P, 2])
        idx = sb("idx", [P, W], I32)
        same = sb("same", [P, W])
        lo = sb("lo", [P, W], BF16)
        hi = sb("hi", [P, W], BF16)
        iota_b = sb("iota_b", [P, P], BF16)
        cnt = sb("cnt", [P, NT])
        hrow = sb("hrow", [P, NT + G], I32)
        psel = sb("psel", [P, NT + G], BF16)
        ident_b = sb("ident_b", [P, P], BF16)
        carry = sb("carry", [P, D])
        carry3 = sb("carry3", [P, 3, D], BF16)
        run = sb("run", [P, E])
        nidx = sb("nidx", [P, G], I32)
        zrow = sb("zrow", [P, D])
        ftab = sb("ftab", [1, 2, FTILES], I32)
        ctab = sb("ctab", [1, E], I32)
        small = sb("small", [P, 8, NT])
        w56 = sb("w56", [P, E, FTILES])

        POOL_WORDS = 22400
        pool = sb("pool", [P, POOL_WORDS])

        class Area:
            def __init__(self):
                self.at = 0

            def take(self, *shape, dt=F32):
                n = 1
                for s in shape:
                    n *= s
                words = n if dt in (F32, I32) else n // 2
                a = pool[:, self.at:self.at + words]
                self.at += words
                assert self.at <= POOL_WORDS, self.at
                if dt != F32:
                    a = a.bitcast(dt)
                if len(shape) > 1:
                    names = "abc"[:len(shape)]
                    a = a.rearrange(f"p ({' '.join(names)}) -> p {' '.join(names)}",
                                    **{k: s for k, s in zip(names, shape)})
                return a

        a0 = Area()
        xn0 = a0.take(G, D)
        xT0 = a0.take(G, DC, P)
        h0 = [a0.take(G, D) for _ in range(2)]
        st0 = a0.take(NT, 6)
        mv0 = a0.take(NT, 2)
        sd0 = a0.take(NT)
        kv = a0.take(SORT_F, dt=I32)
        kd = a0.take(SRC_F, dt=I32)

        a1 = Area()
        ring = a1.take(HALF, D)
        state = [a1.take(HALF, D) for _ in range(2)]
        iblk = [a1.take(HALF, dt=I32) for _ in range(2)]
        fblk = [a1.take(HALF) for _ in range(2)]
        ohl = a1.take(HALF, P, dt=BF16)
        ohh = a1.take(HALF, 50, dt=BF16)[:, :, 0:NT]
        wld = a1.take(DC * H)
        wpk = a1.take(PACK)
        rowa = a1.take(P)
        rowc = a1.take(P)
        diag = a1.take(2, P)
        bT = a1.take(2, P)
        cT = a1.take(2, P)

        a2 = Area()
        end = a2.take(G, D)
        oht = a2.take(G, P, dt=BF16)
        ohs = a2.take(G, P, dt=BF16)
        agg = a2.take(G, D)
        aggT = a2.take(G, D)
        xin = a2.take(G, D)
        xinT = a2.take(G, D)
        rows = [[a2.take(G, ROW) for _ in range(2)] for _ in range(2)]
        st2 = a2.take(G, 6)
        mv2 = a2.take(G, 2)
        sd2 = a2.take(G)
        rs2 = a2.take(G)
        st3 = a2.take(G, 6)
        mv3 = a2.take(G, 2)
        sd3 = a2.take(G)
        rs3 = a2.take(G)
        nb3 = a2.take(G)
        lg = a2.take(G, E)
        ones_of = a2.take(2, G, E)
        rt = [a2.take(G, E) for _ in range(2)]
        masked = a2.take(2, G * E)
        rv = [a2.take(G) for _ in range(6)]
        pos_f = a2.take(2, G)
        rank_sb = a2.take(128)
        pos_i = [a2.take(2, G, dt=I32) for _ in range(2)]
        mk = a2.take(G, E)
        rbase = a2.take(G, E)
        padrow = a2.take(2, ROW)

        a3 = Area()
        spare = X[:, :, :].rearrange("p n d -> p (n d)")
        pk = [spare[:, i * PACK:(i + 1) * PACK] for i in range(XB - 2)] + [a3.take(PACK) for _ in range(2)]
        xs = [a3.take(SUB, ROW) for _ in range(XB)]
        xe = a3.take(DC, FT)
        xeh = a3.take(DC, FT, dt=F16)
        xel = a3.take(DC, FT, dt=F16)
        hf = a3.take(HC, FT)
        hh = a3.take(HC, FT, dt=F16)
        hl = a3.take(HC, FT, dt=F16)
        yt = a3.take(SUB, D)
        yw = a3.take(SUB, D)

        def halves(pack):
            v = pack[:, 0:PK_W].bitcast(F16)
            n = DC * H
            w1h, w1l = (v[:, i * n:(i + 1) * n].rearrange("p (k h) -> p k h", k=DC) for i in (0, 1))
            w2h, w2l = (v[:, i * n:(i + 1) * n].rearrange("p (c d) -> p c d", c=HC) for i in (2, 3))
            return w1h, w1l, w2h, w2l

        s_x = sem("x_loaded")
        s_xt = sem("x_tail_loaded")
        s_zero = sem("x_tail_zeroed")
        s_w = sem("weights_loaded")
        s_cst = sem("constants_loaded")
        s_edge = sem("edges_loaded")
        s_kpad = sem("key_padded")
        s_eps = sem("eps_set")
        s_bn0 = sem("bn0")
        s_mv0 = sem("mv0")
        s_sd0 = sem("sd0")
        s_rs0 = sem("rs0")
        s_nb0 = sem("nb0")
        s_xn0 = sem("xn0")
        s_t0 = sem("t0")
        s_xT0 = sem("xT0")
        s_m0 = sem("m0")
        s_h0 = sem("h0")
        s_b0 = sem("base0")
        s_hst = [sem(f"h_stored{i}") for i in range(2)]
        s_sort = sem("sort_step")
        s_st = sem("sort_turned")
        s_sc = sem("sort_turned_copied")
        s_kout = sem("keys_stored")
        s_kin = sem("keys_dealt")
        s_ext = sem("neighbour_keys_dealt")
        s_edge_t = sem("edge_tables")
        s_blk = sem("index_block")
        s_flag = sem("flag_block")
        s_g = [sem(f"gathered{i}") for i in range(HALF)]
        s_state = sem("state_step")
        s_hist = [sem(f"history_stored{i}") for i in range(2)]
        s_ohh = sem("onehot_hi")
        s_cm = sem("counted")
        s_wl = sem("w_loaded")
        s_hi = sem("w_high")
        s_lo = sem("w_low")
        s_wst = sem("pack_stored")
        s_tab = sem("node_table")
        s_tabm = sem("node_table_mm")
        s_cr = sem("carry_step")
        s_crm = sem("carry_mm")
        s_nblk = sem("node_block")
        s_end = [sem(f"end_gathered{i}") for i in range(G)]
        s_zrow = sem("zeros_set")
        s_zst = sem("zero_row_stored")
        s_oht = sem("oht")
        s_ohT = sem("oht_turned")
        s_ohs = sem("ohs")
        s_cm2 = sem("carry_picked")
        s_agg = sem("agg")
        s_aT = sem("agg_turned")
        s_aTc = sem("aggT")
        s_my = sem("graph_product")
        s_x2 = sem("x2")
        s_bn2 = sem("bn2")
        s_mv2 = sem("mv2")
        s_sd2 = sem("sd2")
        s_rs2 = sem("rs2")
        s_xin = sem("xin")
        s_bn3 = sem("bn3")
        s_mv3 = sem("mv3")
        s_sd3 = sem("sd3")
        s_rs3 = sem("rs3")
        s_nb3 = sem("nb3")
        s_xiT = sem("xin_turned")
        s_xiTc = sem("xinT")
        s_lg = sem("logits")
        s_route = sem("route_step")
        s_exp = sem("exp")
        s_rank = sem("ranks")
        s_row = sem("rows_ready")
        s_scat = [sem(f"rows_scattered{i}") for i in range(2)]
        s_acc0 = sem("acc_started")
        s_ftab = sem("expert_table")
        s_padr = sem("pad_row")
        s_padst = sem("pads_stored")
        s_pk = [sem(f"pack_loaded{i}") for i in range(XB)]
        s_xs = [sem(f"slots_loaded{i}") for i in range(XB)]
        s_fT = sem("f_turned")
        s_xe = sem("xe")
        s_xh = sem("xe_high")
        s_xl = sem("xe_low")
        s_g1 = sem("product1")
        s_gelu = sem("gelu")
        s_hh = sem("h_high")
        s_hl = sem("h_low")
        s_g2 = sem("product2")
        s_yt = sem("y")
        s_yw = sem("y_weighted")
        s_add = sem("y_added")
        s_pool_on = sem("pool_went_on")
        s_v_on = sem("vector_went_on")

        keys = [keyA, keyB]
        h_tiles = h_dram.rearrange("(n p) d -> p n d", p=P)
        acc_tiles = acc.rearrange("(n p) d -> p n d", p=P)
        hist_cols = hist[0:ZERO_ROW, :].rearrange("(f p) d -> p f d", p=P)
        turned_onehots = bank[5][:, :].bitcast(BF16)[:, 0:G * P].rearrange("p (g q) -> p g q", g=G)
        trash_rows = cst[:, C_TRASH:C_TRASH + 2 * NT].rearrange("p (r n) -> p r n", r=2)
        w1_v = w1.rearrange("e (k p) h -> e p k h", p=P)
        w2_v = w2.rearrange("e (c p) d -> e p c d", p=P)

        def all_hidden_stored(eng):
            for par in range(2):
                eng.wait_ge(s_hst[par], 16 * ((NG + 1 - par) // 2))

        def has_place(group, t, lag):
            return group is not None and 0 <= t - lag < G

        def stats(v, a, s_in, st, s_bn, at, t):
            v.wait_ge(s_in, 1 + at + (t + 1))
            v.sem_inc(s_v_on, 1)
            v.bn_stats(st[:, t, :], a).then_inc(s_bn, 1)

        def aggregate(v, st, mv, s_bn, s_mv, at):
            for t in range(G):
                v.wait_ge(s_bn, at + (t + 1))
                v.sem_inc(s_v_on, 1)
                v.bn_aggr(mv[:, t, :], st[:, t, :]).then_inc(s_mv, 1)

        one1, one2 = ones_of[:, 0], ones_of[:, 1]
        tmp, tmp2 = rt
        top1, top2, i1, diff, ex, den = rv
        iota_e = cst[:, C_EXP:C_EXP + G * E].rearrange("p (g e) -> p g e", g=G)

        def wide(a):
            return a.unsqueeze(2).to_broadcast([P, G, E])

        class RouterSteps:
            def __init__(self, v, k, done):
                self.v, self.k, self.n = v, k, done

            def before(self):
                self.v.wait_ge(s_route, 1 + self.k * ROUTE_STEPS + self.n)
                self.n += 1

        def top_two(v, k):
            at = k * G
            c = RouterSteps(v, k, 0)
            v.wait_ge(s_lg, at + G)
            c.before()
            v.tensor_tensor(lg, bank[4][:, 0:G * E].rearrange("p (g e) -> p g e", g=G),
                            br_sb[:, :].unsqueeze(1).to_broadcast([P, G, E]), ALU.add).then_inc(s_route, 1)

            def best(scores, top, onehot):
                c.before()
                v.tensor_reduce(top, scores, AX.X, ALU.max).then_inc(s_route, 1)
                c.before()
                v.tensor_tensor(tmp, scores, wide(top), ALU.is_lt).then_inc(s_route, 1)
                c.before()
                v.scalar_tensor_tensor(out=tmp, in0=tmp, scalar=float(E), in1=iota_e, op0=ALU.mult,
                                       op1=ALU.add).then_inc(s_route, 1)
                c.before()
                v.tensor_reduce(i1, tmp, AX.X, ALU.min).then_inc(s_route, 1)
                c.before()
                v.tensor_tensor(onehot, iota_e, wide(i1), ALU.is_equal).then_inc(s_route, 1)

            best(lg, top1, one1)
            c.before()
            v.scalar_tensor_tensor(out=tmp2, in0=one1, scalar=-3.0e38, in1=lg, op0=ALU.mult,
                                   op1=ALU.add).then_inc(s_route, 1)
            best(tmp2, top2, one2)
            c.before()
            v.tensor_tensor(mk, one1, one2, ALU.add).then_inc(s_route, 1)
            c.before()
            v.tensor_tensor(mk, mk, wide(cst[:, bass.ds(at + C_VALID, G)]), ALU.mult).then_inc(s_route, 1)
            assert c.n == RANK_AT
            c.before()
            v.tensor_tensor(diff, top2, top1, ALU.subtract).then_inc(s_route, 1)
            assert c.n == EXP_AT

        def ranks_out(v, k):
            c = RouterSteps(v, k, EXP_AT)
            v.wait_ge(s_rank, k + 1)
            c.before()
            v.tensor_copy(rank_sb[:, 0:64 + G * E], bank[4][:, 64:128 + G * E]).then_inc(s_route, 1)
            assert c.n == RANKS_OUT
            v.wait_ge(s_route, 1 + k * ROUTE_STEPS + RANKS_OUT)

        def weights_and_rows(v, c, par, t):
            k = c.k
            at = k * G
            if t == 2:
                v.wait_ge(s_exp, k + 1)
                c.before()
                v.tensor_scalar(den, ex, 1.0, None, ALU.add).then_inc(s_route, 1)
            elif t == 3:
                c.before()
                v.reciprocal(den, den).then_inc(s_route, 1)
            elif t == 4:
                c.before()
                v.tensor_copy(rows[par][0][:, :, D + 1], den).then_inc(s_route, 1)
            elif t == 5:
                c.before()
                v.tensor_tensor(rows[par][1][:, :, D + 1], ex, den, ALU.mult).then_inc(s_route, 1)
            elif t < 2:
                c.before()
                v.tensor_scalar(rows[par][t][:, :, D].bitcast(I32), cst[:, bass.ds(at + C_TOKEN, G)], 0.0, None,
                                ALU.add).then_inc(s_route, 1)
            if t == 0:
                c.before()
                v.tensor_copy(rbase[:, 0, :], run[:, :]).then_inc(s_route, 1)
            elif t < G:
                c.before()
                v.tensor_tensor(rbase[:, t, :], rbase[:, t - 1, :], rank_sb[:, 64 + (t - 1) * E:64 + t * E],
                                ALU.add).then_inc(s_route, 1)
            elif t == G:
                c.before()
                v.tensor_tensor(run[:, :], rbase[:, G - 1, :], rank_sb[:, 64 + (G - 1) * E:64 + G * E],
                                ALU.add).then_inc(s_route, 1)
                c.before()
                v.tensor_tensor(rbase, rbase, rank_sb[:, 0:G * E].rearrange("p (g e) -> p g e", g=G),
                                ALU.add).then_inc(s_route, 1)
            elif t == G + 1:
                c.before()
                v.tensor_tensor(masked, ones_of.rearrange("p r g e -> p r (g e)"),
                                rbase.rearrange("p g e -> p (g e)").unsqueeze(1).to_broadcast([P, 2, G * E]),
                                ALU.mult).then_inc(s_route, 1)
            elif t == G + 2:
                c.before()
                v.tensor_reduce(pos_f.rearrange("p r g -> p (r g)"), masked.rearrange("p r (g e) -> p (r g) e", g=G),
                                AX.X, ALU.add).then_inc(s_route, 1)
            elif t == G + 3:
                c.before()
                v.tensor_tensor(pos_f, pos_f, cst[:, bass.ds(at + C_VALID, G)].unsqueeze(1).to_broadcast([P, 2, G]),
                                ALU.mult).then_inc(s_route, 1)
                c.before()
                v.tensor_tensor(pos_i[par], pos_f, trash_rows[:, :, bass.ds(at, G)], ALU.add).then_inc(s_route, 1)
                assert c.n == ROUTE_STEPS, c.n

        from_one = {
            "act": [s_xT0, s_b0, s_ohs, s_aTc, s_xiTc, s_xe],
            "vector": [s_state, s_lo, s_agg, s_x2, s_xin, s_route, s_xl, s_yt],
            "pe": [s_cm],
        }

        block = ctx.enter_context(nc.Block())

        @block.sync
        def _(sp):
            sp.dma_start(cst[:, :], const).then_inc(s_cst, 16)
            sp.dma_start(keyA[0:SRC_P, 0:SRC_F].bitcast(I32),
                         src.rearrange("(p f) -> p f", p=SRC_P)).then_inc(s_edge, 16)
            sp.dma_start(kd[0:SRC_P, :], dst.rearrange("(p f) -> p f", p=SRC_P)).then_inc(s_edge, 16)
            full = (NT - 1) * P
            sp.dma_start(X[:, 0:NT - 1, :], x[0:full, :].rearrange("(n p) d -> p n d", p=P)).then_inc(s_x, 16)
            sp.wait_ge(s_zero, 1)
            sp.dma_start(X[0:TAIL, NT - 1, :], x[full:N_NODES, :]).then_inc(s_xt, 16)
            sp.dma_start(fc_sb[:, :, :], fc.rearrange("(k p) n -> p k n", p=P)).then_inc(s_w, 16)
            sp.dma_start(fcb_sb[:, :], fc_b).then_inc(s_w, 16)
            sp.dma_start(wb_sb[:, :, :], w_bot.rearrange("(k p) n -> p k n", p=P)).then_inc(s_w, 16)
            sp.dma_start(wr_sb[:, :, :], wr.rearrange("(k p) n -> p k n", p=P)).then_inc(s_w, 16)
            sp.dma_start(br_sb[:, :], br).then_inc(s_w, 16)
            sp.wait_ge(s_zrow, 1)
            sp.dma_start(hist[ZERO_ROW:ZERO_ROW + 1, :], zrow[0:1, :]).then_inc(s_zst, 16)
            sp.dma_start(acc[ACC_PAD:ACC_ROWS, :], zrow[:, :]).then_inc(s_acc0, 16)
            for k in range(NG):
                sp.wait_ge(s_h0, G * k + G)
                sp.dma_start(h_tiles[:, k * G:(k + 1) * G, :], h0[k % 2]).then_inc(s_hst[k % 2], 16)
            sp.wait_ge(s_sort, SORT_DONE)
            sp.dma_start(key_dram.rearrange("(p f) -> p f", p=P), keys[SORT_ENDS_IN][:, :]).then_inc(s_kout, 16)
            sp.wait_ge(s_kout, 16)
            sp.dma_start(keyB[:, 0:W], key_dram[0:W * P].rearrange("(p f) -> p f", p=P)).then_inc(s_kin, 16)
            before = key_dram[0:W * (P - 1)].rearrange("(p f) -> p f", f=W)
            with nc.allow_non_contiguous_dma(reason="one key of each partition"):
                sp.dma_start(key_ext[1:P, 0:1], before[:, W - 1:W]).then_inc(s_ext, 16)
                sp.dma_start(key_ext[1:P, 1:2], before[:, 0:1]).then_inc(s_ext, 16)

            def store_history(k, half):
                sp.wait_ge(s_state, 1 + 2 * HALF * k + HALF * (half + 1))
                sp.dma_start(hist_cols[:, bass.ds(2 * HALF * k + HALF * half, HALF), :],
                             state[half]).then_inc(s_hist[half], 16)

            def load_weights(k, part):
                w = w1_v if part == 0 else w2_v
                a = wld.rearrange("p (k h) -> p k h", k=DC if part == 0 else HC)
                sp.wait_ge(s_lo, 1 + 2 * k + part)
                sp.dma_start(a, w[bass.ds(k, 1)].rearrange("e p k h -> p (e k) h")).then_inc(s_wl, 16)

            all_hidden_stored(sp)

            def prepare(k, first=False):
                for part in range(2):
                    t = 2 * k + part
                    load_weights(k, part)
                    if part == 0:
                        if not first:
                            sp.wait_ge(s_wst, 16 * k)
                        sp.dma_start(wpk[:, PK_W:PACK],
                                     params[bass.ds(k, 1)].rearrange("e p n -> p (e n)")).then_inc(s_wl, 16)
                    store_history(t, 0)
                    if part == 1:
                        sp.wait_ge(s_lo, 1 + 2 * k + 2)
                        sp.dma_start(packs[bass.ds(k, 1)].rearrange("e p n -> p (e n)"), wpk).then_inc(s_wst, 16)
                    store_history(t, 1)

            prepare(0, first=True)
            with sp.Fori(1, E) as k:
                prepare(k)
            with sp.Fori(2 * E, GTURNS) as k:
                store_history(k, 0)
                store_history(k, 1)
            sp.wait_ge(s_padr, PAD_STEPS)
            sp.dma_start(slots[E * REGION:E * REGION + FT, :].rearrange("(s p) r -> p s r", p=P),
                         padrow).then_inc(s_padst, 16)
            with sp.Fori(0, NG) as k:
                sp.wait_ge(s_x2, 1 + G * k + G)
                sp.dma_start(acc_tiles[:, bass.ds(k * G, G), :], X[:, bass.ds(k * G, G), :]).then_inc(s_acc0, 16)
            def load_slots(j, b):
                r = sp.value_load(ftab[0:1, 1, bass.ds(j, 1)], min_val=0, max_val=E * REGION)
                sp.dma_start(xs[b], slots[bass.ds(r, FT), :].rearrange("(s p) r -> p s r", p=P)).then_inc(s_xs[b], 16)

            def load_pack(j, b):
                e = sp.value_load(ftab[0:1, 0, bass.ds(j, 1)], min_val=0, max_val=E - 1)
                sp.dma_start(pk[b], packs[bass.ds(e, 1)].rearrange("e p n -> p (e n)")).then_inc(s_pk[b], 16)

            sp.wait_ge(s_ftab, FTAB_STEPS)
            sp.wait_ge(s_acc0, 16 * (NG + 1))
            for e in range(E):
                c = sp.value_load(ctab[0:1, e:e + 1], min_val=0, max_val=(E - 1) * REGION + N_NODES)
                sp.dma_start(slots[bass.ds(c, FT), :].rearrange("(s p) r -> p s r", p=P), padrow).then_inc(s_padst, 16)
            load_pack(0, 0)
            sp.wait_ge(s_padst, 16 * (E + 1))
            for par in range(2):
                sp.wait_ge(s_scat[par], 16 * 2 * G * ((NG + 1 - par) // 2))
            load_slots(0, 0)
            for b in range(1, XB):
                load_slots(b, b)
                load_pack(b, b)
            with sp.Fori(0, FTILES // XB - 1) as t:
                for b in range(XB):
                    sp.wait_ge(s_yt, 1 + SUB * (t * XB + b) + SUB)
                    load_pack(t * XB + (b + XB), b)
                    sp.wait_ge(s_add, 16 * SUB * (t * XB + b) + 16 * SUB)
                    load_slots(t * XB + (b + XB), b)
            sp.wait_ge(s_add, 16 * SUB * FTILES)
            all_hidden_stored(sp)
            sp.wait_ge(s_wst, 16 * E)
            sp.wait_ge(s_acc0, 16 * (NG + 1))

        @block.gpsimd
        def _(pool_e):
            h_bound = pool_e.to_reg(NT * P - 1)
            hist_bound = pool_e.to_reg(ZERO_ROW)
            slot_bound = pool_e.to_reg(SLOT_ROWS - 1)
            acc_bound = pool_e.to_reg(ACC_ROWS - 1)
            all_hidden_stored(pool_e)

            def gather_half(k, half, first=False):
                pool_e.wait_ge(s_blk, 2 * k + (half + 1))
                pool_e.sem_inc(s_pool_on, 1)
                for u in range(HALF):
                    if not first:
                        pool_e.wait_ge(s_state, 1 + 2 * HALF * k + (HALF * (half - 1) + u + 1))
                        pool_e.sem_inc(s_pool_on, 1)
                    pool_e.indirect_dma_start(
                        ring[:, u, :], None, h_dram, bass.IndirectOffsetOnAxis(iblk[half][:, u:u + 1], 0),
                        bounds_check=h_bound, oob_is_err=True).then_inc(s_g[u], 16)

            gather_half(0, 0, first=True)
            gather_half(0, 1)
            with pool_e.Fori(1, GTURNS) as k:
                gather_half(k, 0)
                gather_half(k, 1)

            def gather_ends(k):
                pool_e.wait_ge(s_nblk, k + 1)
                pool_e.wait_ge(s_agg, 1 + k * G)
                pool_e.sem_inc(s_pool_on, 1)
                for t in range(G):
                    pool_e.indirect_dma_start(
                        end[:, t, :], None, hist, bass.IndirectOffsetOnAxis(nidx[:, t:t + 1], 0),
                        bounds_check=hist_bound, oob_is_err=True).then_inc(s_end[t], 16)

            def scatter_rows(j, par):
                k = 2 * j + par
                pool_e.wait_ge(s_route, 1 + (k + 1) * ROUTE_STEPS)
                for r in range(2):
                    for t in range(G):
                        pool_e.wait_ge(s_row, k * (G + 1) + (t + 1 if r == 0 else G + 1))
                        pool_e.sem_inc(s_pool_on, 1)
                        pool_e.indirect_dma_start(
                            slots, bass.IndirectOffsetOnAxis(pos_i[par][:, r, t:t + 1], 0), rows[par][r][:, t, :], None,
                            bounds_check=slot_bound, oob_is_err=True).then_inc(s_scat[par], 16)

            pool_e.wait_ge(s_hist[0], 16 * GTURNS)
            pool_e.wait_ge(s_hist[1], 16 * GTURNS)
            pool_e.wait_ge(s_zst, 16)
            gather_ends(0)
            for k in range(1, 3):
                gather_ends(k)
            with pool_e.Fori(0, (NG - 3) // 2) as j:
                for par in range(2):
                    gather_ends(2 * j + par + 3)
                    scatter_rows(j, par)
            for k in range(NG - 3, NG):
                scatter_rows(k // 2, k % 2)

            pool_e.wait_ge(s_acc0, 16 * (NG + 1))

            def add_rows(t, first=False):
                for b in range(XB):
                    for s in range(SUB):
                        pool_e.wait_ge(s_yw, SUB * (t * XB + b) + (s + 1))
                        if not (first and b == 0 and s == 0):
                            pool_e.wait_ge(s_add, 16 * (SUB * (t * XB + b) + s))
                        pool_e.sem_inc(s_pool_on, 1)
                        pool_e.indirect_dma_start(
                            acc, bass.IndirectOffsetOnAxis(xs[b][:, s, D:D + 1].bitcast(I32), 0), yw[:, s, :], None,
                            bounds_check=acc_bound, oob_is_err=True, compute_op=ALU.add).then_inc(s_add, 16)

            add_rows(0, first=True)
            with pool_e.Fori(1, FTILES // XB) as t:
                add_rows(t)

        @block.scalar
        def _(act):
            for s in from_one["act"]:
                act.sem_inc(s, 1)
            def normalize0(k, t):
                n = k * G + t
                act.activation(xn0[:, t, :], X[:, bass.ds(n, 1), :].rearrange("p n d -> p (n d)"), ACT.Identity,
                               bias=nb0[:, bass.ds(n, 1)], scale=rs0[:, bass.ds(n, 1)]).then_inc(s_xn0, 1)

            def turned0(k, t):
                act.wait_ge(s_t0, k * G + (t + 1))
                act.copy(xT0[:, t, :, :].rearrange("p k q -> p (k q)"), bank[t % 2][:, 0:D]).then_inc(s_xT0, 1)

            def hidden(k, t):
                n = k * G + t
                act.wait_ge(s_m0, k * G + (t + 1))
                if t == 0 and k >= 2:
                    act.wait_ge(s_hst[k % 2], 16 * (k // 2))
                act.activation(h0[k % 2][:, t, :], bank[2 + t % 3][:, 0:D], ACT.Relu).then_inc(s_h0, 1)
                act.activation(X[:, bass.ds(n, 1), :].rearrange("p n d -> p (n d)"), bank[2 + t % 3][:, D:2 * D],
                               ACT.Copy).then_inc(s_b0, 1)

            def tiles0(tiles):
                for k, t in tiles[:2]:
                    normalize0(k, t)
                for i, (k, t) in enumerate(tiles):
                    turned0(k, t)
                    if i >= 1:
                        hidden(*tiles[i - 1])
                    if i + 2 < len(tiles):
                        normalize0(*tiles[i + 2])
                hidden(*tiles[-1])

            act.wait_ge(s_mv0, NT)
            act.wait_ge(s_eps, 1)
            act.activation(sd0, mv0[:, :, 1], ACT.Sqrt, bias=eps[:, 0:1]).then_inc(s_sd0, 1)
            act.wait_ge(s_nb0, 1)
            for k in range(EARLY):
                tiles0([(k, t) for t in range(G)])
            for m, tiles in enumerate(LATE_TILES):
                to = keys[1 - SORT_TURN_FROM[m]]
                for q in range(2 - m % 2):
                    act.wait_ge(s_st, 2 * m + q + 1)
                    act.copy(to[:, q * 512:(q + 1) * 512], bank[5 + q][:, :]).then_inc(s_sc, 1)
                if tiles:
                    tiles0(tiles)

            def blocks(k, half):
                act.wait_ge(s_state, 1 + 2 * HALF * k + HALF * (half - 1))
                at = 2 * HALF * k + HALF * half
                act.copy(iblk[half], idx[:, bass.ds(at, HALF)]).then_inc(s_blk, 1)
                act.copy(fblk[half], same[:, bass.ds(at, HALF)]).then_inc(s_flag, 1)

            def high(k, part):
                w1h, w1l, w2h, w2l = halves(wpk)
                dst_ = w1h if part == 0 else w2h
                a = wld.rearrange("p (k h) -> p k h", k=DC if part == 0 else HC)
                act.wait_ge(s_wl, 48 * k + (32 if part == 0 else 48))
                act.activation(dst_, a, ACT.Copy, scale=WS).then_inc(s_hi, 1)

            act.wait_ge(s_edge_t, 1)
            all_hidden_stored(act)
            for half in range(2):
                act.copy(iblk[half], idx[:, half * HALF:(half + 1) * HALF]).then_inc(s_blk, 1)
            act.wait_ge(s_edge_t, EDGE_STEPS)
            for half in range(2):
                act.copy(fblk[half], same[:, half * HALF:(half + 1) * HALF]).then_inc(s_flag, 1)
            high(0, 0)
            blocks(1, 0)
            blocks(1, 1)
            high(0, 1)
            with act.Fori(1, E) as k:
                for part in range(2):
                    blocks(2 * k + part, 0)
                    blocks(2 * k + part, 1)
                    high(k, part)
            with act.Fori(2 * E, GTURNS) as k:
                blocks(k, 0)
                blocks(k, 1)
            act.wait_ge(s_tab, TAB_STEPS)
            act.copy(nidx[:, :], hrow[:, 0:G]).then_inc(s_nblk, 1)
            act.wait_ge(s_crm, 2)
            act.copy(carry[:, :], bank[7][:, 0:D]).then_inc(s_cr, 1)


            def onehots_copied(k):
                act.wait_ge(s_ohT, k + 1)
                act.copy(ohs, turned_onehots).then_inc(s_ohs, 1)

            def graph_turned(k, t):
                act.wait_ge(s_aT, k * G + (t + 1))
                act.copy(aggT[:, t, :], bank[1][:, 0:D]).then_inc(s_aTc, 1)

            def input_turned(k, t):
                act.wait_ge(s_xiT, k * G + (t + 1))
                act.copy(xinT[:, t, :], bank[0][:, 0:D]).then_inc(s_xiTc, 1)

            def next_ends(k):
                act.wait_ge(s_agg, 1 + k * G)
                act.copy(nidx[:, :], hrow[:, bass.ds(k * G, G)]).then_inc(s_nblk, 1)

            def deviation2(k):
                act.wait_ge(s_mv2, k * G + G)
                act.activation(sd2, mv2[:, :, 1], ACT.Sqrt, bias=eps[:, 0:1]).then_inc(s_sd2, 1)

            def deviation3(k):
                act.wait_ge(s_mv3, k * G + G)
                act.activation(sd3, mv3[:, :, 1], ACT.Sqrt, bias=eps[:, 0:1]).then_inc(s_sd3, 1)

            def expert_rows(j, par, first=False):
                k = 2 * j + par
                act.wait_ge(s_nb3, k + 1)
                if not first:
                    act.wait_ge(s_scat[par], 16 * 2 * G * j)
                for t in range(G):
                    act.activation(rows[par][0][:, t, 0:D], xin[:, t, :], ACT.Identity, bias=nb3[:, t:t + 1],
                                   scale=rs3[:, t:t + 1]).then_inc(s_row, 1)
                act.wait_ge(s_route, 1 + k * ROUTE_STEPS + EXP_AT)
                act.activation(ex, diff, ACT.Exp).then_inc(s_exp, 1)

            def second_rows(k, par):
                act.wait_ge(s_row, k * (G + 1) + G)
                act.copy(rows[par][1][:, :, 0:D], rows[par][0][:, :, 0:D]).then_inc(s_row, 1)

            def tiles_of(back, front, routed=None, par=None):
                for t in range(G + 1):
                    if routed is not None and t == 2:
                        second_rows(routed, par)
                    if has_place(back, t, 0):
                        input_turned(back, t)
                    if has_place(front, t, 1):
                        graph_turned(front, t - 1)
                act.activation(warm[:, :], eps[:, :], ACT.Sqrt)

            def two_groups(j, first=False):
                for par in range(2):
                    k = 2 * j + par
                    if first and par == 0:
                        tiles_of(k, k + 1)
                    else:
                        tiles_of(k, k + 1, k - 1, 1 - par)
                    next_ends(k + 2)
                    deviation3(k)
                    deviation2(k + 1)
                    onehots_copied(k + 2)
                    expert_rows(j, par, first)

            onehots_copied(0)
            tiles_of(None, 0)
            next_ends(1)
            deviation2(0)
            onehots_copied(1)
            two_groups(0, first=True)
            with act.Fori(1, NG // 2) as j:
                two_groups(j)
            tiles_of(NG - 1, None, NG - 2, 1)
            deviation3(NG - 1)
            expert_rows(NG // 2, 0)
            second_rows(NG - 1, 0)

            def inputs(k, b, nxt=0):
                j = k * XB + b
                act.wait_ge(s_pk[b], 16 * k + 16)
                act.wait_ge(s_fT, j + 1)
                act.wait_ge(s_xl, 1 + j)
                for c in range(DC):
                    act.activation(xe[:, c, :], bank[0][:, c * FT:(c + 1) * FT], ACT.Identity,
                                   bias=pk[b][:, PK_B + c:PK_B + c + 1],
                                   scale=pk[b][:, PK_G + c:PK_G + c + 1]).then_inc(s_xe, 1)

            def gelus(k, b):
                j = k * XB + b
                for c in range(HC):
                    act.wait_ge(s_g1, HC * j + (2 * (c // 2) + 2))
                    act.activation(hf[:, c, :], bank[1 + c // 2][:, (c % 2) * FT:(c % 2 + 1) * FT], ACT.Gelu,
                                   bias=pk[b][:, PK_B1 + c:PK_B1 + c + 1], scale=1.0 / WS).then_inc(s_gelu, 1)

            inputs(0, 0)
            with act.Fori(0, FTILES // XB - 1) as k:
                for b in range(XB):
                    gelus(k, b)
                    inputs(k + (b + 1) // XB, (b + 1) % XB)
            for b in range(XB):
                gelus(FTILES // XB - 1, b)
                if b + 1 < XB:
                    inputs(FTILES // XB - 1, b + 1)

        @block.tensor
        def _(pe):
            for s in from_one["pe"]:
                pe.sem_inc(s, 1)
            pe.wait_ge(s_w, 16 * 5)
            pe.wait_ge(s_cst, 16)

            def turn0(k, t):
                pe.wait_ge(s_xn0, k * G + (t + 1))
                pe.wait_ge(s_xT0, 1 + k * G + max(t - 1, 0))
                for c in range(DC):
                    mm = pe.transpose(bank[t % 2][:, c * P:(c + 1) * P], xn0[:, t, c * P:(c + 1) * P], ident)
                mm.then_inc(s_t0, 1)

            def product0(k, t):
                pe.wait_ge(s_xT0, 1 + k * G + (t + 1))
                pe.wait_ge(s_b0, 1 + k * G + max(t - 2, 0))
                b = bank[2 + t % 3]
                n = k * G + t
                for c in range(DC):
                    pe.matmul(b[:, :], xT0[:, t, c, :], fc_sb[:, c, :], start=c == 0, stop=False)
                pe.matmul(b[:, 0:D], ones[0:1, :], fcb_sb[:, :], start=False, stop=False)
                pe.matmul(b[:, D:2 * D], ident, X[:, bass.ds(n, 1), :].rearrange("p n d -> p (n d)"),
                          start=False, stop=True).then_inc(s_m0, 1)

            def tiles0(tiles):
                for i, (k, t) in enumerate(tiles):
                    turn0(k, t)
                    if i >= 1:
                        product0(*tiles[i - 1])
                product0(*tiles[-1])

            with pe.Fori(0, EARLY) as k:
                tiles0([(k, t) for t in range(G)])

            for m in range(2 * (LEVELS - FREE_LEVELS)):
                pe.wait_ge(s_sort, SORT_TURN_AT[m])
                fr = keys[SORT_TURN_FROM[m]]
                for q in range(2):
                    for c in range(4):
                        cc = 4 * q + c
                        mm = pe.transpose(bank[5 + q][:, c * P:(c + 1) * P], fr[:, cc * P:(cc + 1) * P], ident)
                    mm.then_inc(s_st, 1)
                if LATE_TILES[m]:
                    tiles0(LATE_TILES[m])

            def count(k, half, first=False, last=False):
                pe.wait_ge(s_ohh, 2 * k + (half + 1))
                for u in range(HALF):
                    mm = pe.matmul(bank[7][:, 0:NT], ohl[:, u, :], ohh[:, u, :],
                                   start=first and u == 0, stop=last and u == HALF - 1)
                mm.then_inc(s_cm, 1)

            count(0, 0, first=True)
            count(0, 1)
            with pe.Fori(1, GTURNS - 1) as k:
                count(k, 0)
                count(k, 1)
            count(GTURNS - 1, 0)
            count(GTURNS - 1, 1, last=True)

            pe.wait_ge(s_tab, 1)
            pe.matmul(bank[6][:, 0:NT], tri, cnt[:, :], start=True, stop=True)
            pe.matmul(bank[6][:, 64:64 + NT], ones, cnt[:, :], start=True, stop=True).then_inc(s_tabm, 1)
            pe.wait_ge(s_state, 1 + 2 * HALF * GTURNS)
            pe.wait_ge(s_cr, CR_DIAG)
            for c in range(DC):
                pe.transpose(bank[4][:, c * P:(c + 1) * P], state[1][:, HALF - 1, c * P:(c + 1) * P], ident)
            for c in range(2):
                mm = pe.matmul(bank[5][:, c * P:(c + 1) * P], ones, diag[:, c, :], start=True, stop=True)
            mm.then_inc(s_crm, 1)
            pe.wait_ge(s_cr, CR_DONE)
            for c in range(DC):
                mm = pe.transpose(bank[7][:, c * P:(c + 1) * P], cT[:, c, :], ident)
            mm.then_inc(s_crm, 1)
            pe.wait_ge(s_cr, CR_SPLIT)
            pe.wait_ge(s_tab, TAB_STEPS)

            def turn_onehots(k):
                pe.wait_ge(s_oht, k + 1)
                pe.wait_ge(s_ohs, 1 + k)
                for t in range(G):
                    mm = pe.transpose(turned_onehots[:, t, :], oht[:, t, :], ident_b[:, :])
                mm.then_inc(s_ohT, 1)

            def pick(k, t):
                pe.wait_ge(s_ohs, 1 + (k + 1))
                pe.wait_ge(s_agg, 1 + k * G + max(t - 1, 0))
                for i in range(3):
                    mm = pe.matmul(bank[2 + t % 2][:, 0:D], ohs[:, t, :], carry3[:, i, :], start=i == 0, stop=i == 2)
                mm.then_inc(s_cm2, 1)

            def turn_aggregate(k, t):
                pe.wait_ge(s_agg, 1 + k * G + (t + 1))
                pe.wait_ge(s_aTc, 1 + k * G + t)
                for c in range(DC):
                    mm = pe.transpose(bank[1][:, c * P:(c + 1) * P], agg[:, t, c * P:(c + 1) * P], ident)
                mm.then_inc(s_aT, 1)

            def graph(k, t):
                pe.wait_ge(s_aTc, 1 + k * G + (t + 1))
                pe.wait_ge(s_x2, 1 + k * G + max(t - 1, 0))
                for c in range(DC):
                    mm = pe.matmul(bank[6 + t % 2][:, 0:D], aggT[:, t, c * P:(c + 1) * P], wb_sb[:, c, :],
                                   start=c == 0, stop=c == DC - 1)
                mm.then_inc(s_my, 1)

            def turn_input(k, t):
                pe.wait_ge(s_xin, 1 + k * G + (t + 1))
                pe.wait_ge(s_xiTc, 1 + k * G + t)
                for c in range(DC):
                    mm = pe.transpose(bank[0][:, c * P:(c + 1) * P], xin[:, t, c * P:(c + 1) * P], ident)
                mm.then_inc(s_xiT, 1)

            def logits(k, t):
                pe.wait_ge(s_xiTc, 1 + k * G + (t + 1))
                for c in range(DC):
                    mm = pe.matmul(bank[4][:, t * E:(t + 1) * E], xinT[:, t, c * P:(c + 1) * P], wr_sb[:, c, :],
                                   start=c == 0, stop=c == DC - 1)
                mm.then_inc(s_lg, 1)

            def ranks(k):
                pe.wait_ge(s_route, 1 + k * ROUTE_STEPS + RANK_AT)
                pe.matmul(bank[4][:, 64:64 + G * E], tri, mk.rearrange("p g e -> p (g e)"), start=True, stop=True)
                pe.matmul(bank[4][:, 128:128 + G * E], ones, mk.rearrange("p g e -> p (g e)"),
                          start=True, stop=True).then_inc(s_rank, 1)

            def tiles_of(back, front):
                for t in range(-1, G + 2):
                    if has_place(back, t, 0):
                        turn_input(back, t)
                    if has_place(front, t, -1):
                        pick(front, t + 1)
                    if has_place(back, t, 1):
                        logits(back, t - 1)
                    if has_place(front, t, 1):
                        turn_aggregate(front, t - 1)
                    if has_place(front, t, 2):
                        graph(front, t - 2)

            turn_onehots(0)
            tiles_of(None, 0)
            turn_onehots(1)
            with pe.Fori(0, NG - 1) as k:
                tiles_of(k, k + 1)
                turn_onehots(k + 2)
                ranks(k)
            tiles_of(NG - 1, None)
            ranks(NG - 1)

            def turn(k, b):
                j = k * XB + b
                pe.wait_ge(s_xs[b], 16 * k + 16)
                pe.wait_ge(s_xe, 1 + DC * j)
                for c in range(DC):
                    for s in range(SUB):
                        mm = pe.transpose(bank[0][:, c * FT + s * P:c * FT + (s + 1) * P],
                                          xs[b][:, s, c * P:(c + 1) * P], ident)
                mm.then_inc(s_fT, 1)

            def product1(k, b):
                j = k * XB + b
                w1h, w1l, _, _ = halves(pk[b])
                pe.wait_ge(s_xl, 1 + j + 1)
                pe.wait_ge(s_pk[b], 16 * k + 16)
                for h in range(HC):
                    o = bank[1 + h // 2][:, (h % 2) * FT:(h % 2 + 1) * FT]
                    n = 0
                    for c in range(DC):
                        for w, a in ((w1h, xeh), (w1h, xel), (w1l, xeh)):
                            mm = pe.matmul(o, w[:, c, h * P:(h + 1) * P], a[:, c, :],
                                           start=n == 0, stop=n == 3 * DC - 1)
                            n += 1
                    mm.then_inc(s_g1, 1)

            def product2(k, b):
                j = k * XB + b
                _, _, w2h, w2l = halves(pk[b])
                pe.wait_ge(s_yt, 1 + SUB * j)
                for h in range(HC):
                    if h % 2 == 0:
                        pe.wait_ge(s_hl, (HC // 2) * j + (h // 2 + 1))
                    for s in range(SUB):
                        for i, (a, w) in enumerate(((hh, w2h), (hh, w2l), (hl, w2h))):
                            mm = pe.matmul(bank[5 + s][:, 0:D], a[:, h, s * P:(s + 1) * P], w[:, h, :],
                                           start=h == 0 and i == 0, stop=h == HC - 1 and i == 2)
                        if h == HC - 1:
                            mm.then_inc(s_g2, 1)

            turn(0, 0)
            with pe.Fori(0, FTILES // XB - 1) as k:
                for b in range(XB):
                    product1(k, b)
                    turn(k + (b + 1) // XB, (b + 1) % XB)
                    product2(k, b)
            for b in range(XB):
                product1(FTILES // XB - 1, b)
                if b + 1 < XB:
                    turn(FTILES // XB - 1, b + 1)
                product2(FTILES // XB - 1, b)

        @block.vector
        def _(v):
            for s in from_one["vector"]:
                v.sem_inc(s, 1)
            v.memset(X[:, NT - 1, :], 0.0).then_inc(s_zero, 1)
            v.memset(eps[:, :], EPS).then_inc(s_eps, 1)
            v.memset(zrow[:, :], 0.0).then_inc(s_zrow, 1)
            v.memset(kv.bitcast(F32), 512.0).then_inc(s_kpad, 1)
            v.memset(key_ext[:, :], 512.0).then_inc(s_kpad, 1)
            n = [0]

            def step(ins, wait=True):
                n[0] += 1
                ins.then_inc(s_sort, 1)
                if wait:
                    v.wait_ge(s_sort, n[0])

            v.wait_ge(s_cst, 16)
            v.wait_ge(s_edge, 32)
            v.wait_ge(s_kpad, 2)
            ks = keyA[0:SRC_P, 0:SRC_F].bitcast(I32)
            kb = keyB[0:SRC_P, 0:SRC_F].bitcast(I32)
            step(v.tensor_scalar(kb, ks, DST_BITS, None, ALU.logical_shift_left))
            step(v.tensor_tensor(ks, kb, kd[0:SRC_P, :], ALU.bitwise_or))
            step(v.tensor_scalar(kv[0:SRC_P, 0:SRC_F], ks, 1 << 30, None, ALU.bitwise_or))
            step(v.tensor_scalar(keyA[:, :], kv.bitcast(F32), cst[:, C_SIGN:C_SIGN + 1], None, ALU.mult))

            cur, nxt = keyA, keyB

            def split(a, j):
                return a[:, :].rearrange("p (n t j) -> p n t j", t=2, j=j)

            def exchange(j, mirror=False):
                nonlocal cur, nxt
                a, b = split(cur, j), split(nxt, j)
                if mirror:
                    low, high_r = a[:, :, 0, :], a[:, :, 1, ::-1]
                    high, low_r = a[:, :, 1, :], a[:, :, 0, ::-1]
                else:
                    low, high_r = a[:, :, 0, :], a[:, :, 1, :]
                    high, low_r = high_r, low
                step(v.tensor_tensor(b[:, :, 0, :], low, high_r, ALU.min), wait=False)
                step(v.tensor_tensor(b[:, :, 1, :], high, low_r, ALU.max))
                cur, nxt = nxt, cur

            def moments0():
                v.wait_ge(s_x, 16)
                v.wait_ge(s_xt, 16)
                with v.Fori(0, NG) as k:
                    for t in range(G):
                        v.bn_stats(st0[:, bass.ds(k * G + t, 1), :].rearrange("p n s -> p (n s)"),
                                   X[:, bass.ds(k * G + t, 1), :].rearrange("p n d -> p (n d)")).then_inc(s_bn0, 1)
                v.wait_ge(s_bn0, NT)
                for n_ in range(NT):
                    v.bn_aggr(mv0[:, n_, :], st0[:, n_, :]).then_inc(s_mv0, 1)

            def scales0():
                v.wait_ge(s_sd0, 1)
                v.reciprocal(rs0[:, :], sd0).then_inc(s_rs0, 1)
                v.wait_ge(s_rs0, 1)
                v.scalar_tensor_tensor(out=nb0[:, :], in0=mv0[:, :, 0], scalar=-1.0, in1=rs0[:, :], op0=ALU.mult,
                                       op1=ALU.mult).then_inc(s_nb0, 1)

            for lv in range(1, FREE_LEVELS + 1):
                if lv == 6:
                    moments0()
                exchange(1 << (lv - 1), mirror=True)
                if lv == 6:
                    scales0()
                for d in reversed(range(lv - 1)):
                    exchange(1 << d)

            def after_turn(m, j):
                nonlocal cur, nxt
                cur, nxt = nxt, cur
                copied = 3 * (m // 2) + 2 * (m % 2)
                if m % 2 == 1:
                    v.wait_ge(s_sc, copied + 1)
                    v.wait_ge(s_st, 2 * m + 2)
                    low, high = cur[:, 0:j], bank[6][:, :]
                    step(v.tensor_tensor(nxt[:, 0:j], low, high, ALU.min), wait=False)
                    step(v.tensor_tensor(nxt[:, j:2 * j], high, low, ALU.max))
                else:
                    for q in range(2):
                        v.wait_ge(s_sc, copied + q + 1)
                        a, b = (z[:, q * 512:(q + 1) * 512].rearrange("p (n t j) -> p n t j", t=2, j=j)
                                for z in (cur, nxt))
                        step(v.tensor_tensor(b[:, :, 0, :], a[:, :, 0, :], a[:, :, 1, :], ALU.min), wait=False)
                        step(v.tensor_tensor(b[:, :, 1, :], a[:, :, 1, :], a[:, :, 0, :], ALU.max), wait=q == 1)
                cur, nxt = nxt, cur

            turns = 0
            for lv in range(FREE_LEVELS + 1, LEVELS + 1):
                j = C_SIGN + lv - FREE_LEVELS
                step(v.tensor_scalar(nxt[:, :], cur[:, :], cst[:, j:j + 1], None, ALU.mult))
                cur, nxt = nxt, cur
                for m in (lv - FREE_LEVELS, FREE_LEVELS):
                    assert n[0] == SORT_TURN_AT[turns] and cur is keys[SORT_TURN_FROM[turns]]
                    after_turn(turns, 1 << (m - 1))
                    turns += 1
                    for d in reversed(range(m - 1)):
                        exchange(1 << d)
            assert cur is keys[SORT_ENDS_IN]
            assert n[0] == SORT_DONE, n[0]

            m = [0]

            def tab(ins, wait=True):
                m[0] += 1
                ins.then_inc(s_edge_t, 1)
                if wait:
                    v.wait_ge(s_edge_t, m[0])

            v.wait_ge(s_kin, 16)
            kw = keyB[:, 0:W].bitcast(I32)
            sk = keyA[:, 0:W].bitcast(I32)
            ext = small[:, 0, 0:2].bitcast(I32)
            SRC_MASK = (1 << 14) - 1
            tab(v.tensor_scalar(idx[:, :], kw, (1 << DST_BITS) - 1, None, ALU.bitwise_and), wait=False)
            all_hidden_stored(v)
            v.wait_ge(s_ext, 32)
            tab(v.tensor_scalar(sk, kw, DST_BITS, SRC_MASK, ALU.logical_shift_right, ALU.bitwise_and), wait=False)
            tab(v.tensor_scalar(ext, key_ext[:, :].bitcast(I32), DST_BITS, SRC_MASK, ALU.logical_shift_right,
                                ALU.bitwise_and), wait=False)
            tab(v.memset(same[:, 0:1], 0.0), wait=False)
            tab(v.memset(state[1][:, HALF - 1, :], 0.0), wait=False)
            tab(v.tensor_copy(iota_b[:, :], iota))
            tab(v.tensor_tensor(same[:, 1:W], sk[:, 1:W], sk[:, 0:W - 1], ALU.is_equal), wait=False)
            tab(v.tensor_tensor(small[:, 1, 0:1], sk[:, 0:1], ext[:, 0:1], ALU.is_equal), wait=False)
            tab(v.tensor_tensor(small[:, 1, 1:2], ext[:, 1:2], ext[:, 0:1], ALU.is_equal), wait=False)
            tab(v.tensor_scalar(kw, sk, 127, None, ALU.bitwise_and))
            tab(v.tensor_copy(lo[:, :], kw))
            tab(v.tensor_scalar(kw, sk, 7, None, ALU.logical_shift_right))
            tab(v.tensor_copy(hi[:, :], kw))
            assert m[0] == EDGE_STEPS, m[0]

            def onehots(k, half):
                at = 2 * HALF * k + HALF * half
                v.wait_ge(s_cm, 1 + 2 * k + half)
                v.tensor_tensor(ohl, iota_b[:, :].unsqueeze(1).to_broadcast([P, HALF, P]),
                                lo[:, bass.ds(at, HALF)].unsqueeze(2).to_broadcast([P, HALF, P]), ALU.is_equal)
                v.tensor_tensor(ohh, iota_b[:, 0:NT].unsqueeze(1).to_broadcast([P, HALF, NT]),
                                hi[:, bass.ds(at, HALF)].unsqueeze(2).to_broadcast([P, HALF, NT]),
                                ALU.is_equal).then_inc(s_ohh, 1)

            def scan(k, half, first=False, part=range(HALF)):
                for u in part:
                    if u == 0:
                        v.wait_ge(s_flag, 2 * k + half + 1)
                        if not first:
                            v.wait_ge(s_hist[half], 16 * k)
                    v.wait_ge(s_g[u], 32 * k + 16 * (half + 1))
                    v.wait_ge(s_state, 1 + 2 * HALF * k + (HALF * half + u))
                    prev = state[half][:, u - 1, :] if u else state[1 - half][:, HALF - 1, :]
                    v.scalar_tensor_tensor(out=state[half][:, u, :], in0=prev, scalar=fblk[half][:, u:u + 1],
                                           in1=ring[:, u, :], op0=ALU.mult, op1=ALU.max).then_inc(s_state, 1)

            def low(k, part):
                w1h, w1l, w2h, w2l = halves(wpk)
                hi_, lo_ = (w1h, w1l) if part == 0 else (w2h, w2l)
                a = wld.rearrange("p (k h) -> p k h", k=DC if part == 0 else HC)
                v.wait_ge(s_hi, 2 * k + part + 1)
                v.scalar_tensor_tensor(out=lo_, in0=a, scalar=WS, in1=hi_, op0=ALU.mult,
                                       op1=ALU.subtract).then_inc(s_lo, 1)

            def turns(k, first=False):
                for part in range(2):
                    t = 2 * k + part
                    onehots(t, 0)
                    scan(t, 0, first and part == 0)
                    low(k, part)
                    onehots(t, 1)
                    scan(t, 1, first and part == 0)

            turns(0, first=True)
            with v.Fori(1, E) as k:
                turns(k)
            with v.Fori(2 * E, GTURNS - 1) as k:
                for half in range(2):
                    onehots(k, half)
                    scan(k, half)
            onehots(GTURNS - 1, 0)
            scan(GTURNS - 1, 0)
            onehots(GTURNS - 1, 1)
            scan(GTURNS - 1, 1, part=range(1))

            c = [0]

            def nt(ins, wait=True):
                c[0] += 1
                ins.then_inc(s_tab, 1)
                if wait:
                    v.wait_ge(s_tab, c[0])

            start, tot, endp, pe_, ps_, nz, fe = (small[:, i, :] for i in (2, 3, 4, 5, 6, 7, 0))
            v.wait_ge(s_cm, 1 + 2 * GTURNS)
            nt(v.tensor_copy(cnt[:, :], bank[7][:, 0:NT]))
            v.wait_ge(s_tabm, 1)
            nt(v.tensor_copy(fe, bank[6][:, 64:64 + NT]))
            nt(v.tensor_tensor_scan(tot, ones[:, 0:NT], fe, 0.0, ALU.mult, ALU.add))
            nt(v.tensor_tensor(tot, tot, fe, ALU.subtract))
            nt(v.tensor_tensor(start, bank[6][:, 0:NT], tot, ALU.add))
            nt(v.scalar_tensor_tensor(out=endp, in0=cnt[:, :], scalar=-1.0, in1=start, op0=ALU.add, op1=ALU.add),
               wait=False)
            nt(v.tensor_scalar(nz, cnt[:, :], 0.0, None, ALU.is_gt))
            ROUND = 12582912.0
            for o, i in ((pe_, endp), (ps_, start)):
                nt(v.tensor_scalar(o, i, 0.5, 1.0 / W, ALU.add, ALU.mult))
                nt(v.tensor_scalar(o, o, -0.5, ROUND, ALU.add, ALU.add))
                nt(v.tensor_scalar(o, o, ROUND, None, ALU.subtract))
            nt(v.scalar_tensor_tensor(out=fe, in0=pe_, scalar=-float(W), in1=endp, op0=ALU.mult, op1=ALU.add))
            nt(v.scalar_tensor_tensor(out=fe, in0=fe, scalar=float(P), in1=pe_, op0=ALU.mult, op1=ALU.add))
            nt(v.scalar_tensor_tensor(out=fe, in0=fe, scalar=-float(ZERO_ROW), in1=nz, op0=ALU.add, op1=ALU.mult))
            nt(v.tensor_scalar(hrow[:, 0:NT], fe, float(ZERO_ROW), None, ALU.add))
            nt(v.memset(hrow[:, NT:NT + G], 0))
            nt(v.tensor_tensor(ps_, pe_, ps_, ALU.is_gt))
            nt(v.tensor_tensor(ps_, ps_, nz, ALU.mult))
            nt(v.scalar_tensor_tensor(out=fe, in0=pe_, scalar=1.0, in1=ps_, op0=ALU.add, op1=ALU.mult))
            nt(v.tensor_scalar(psel[:, 0:NT], fe, -1.0, None, ALU.add), wait=False)
            nt(v.memset(psel[:, NT:NT + G], -1.0), wait=False)
            nt(v.tensor_copy(ident_b[:, :], ident))
            assert c[0] == TAB_STEPS, c[0]
            scan(GTURNS - 1, 1, part=range(1, HALF))

            r = [0]

            def cr(ins, wait=True):
                r[0] += 1
                ins.then_inc(s_cr, 1)
                if wait:
                    v.wait_ge(s_cr, r[0])

            cr(v.tensor_tensor(small[:, 1, 2:3], small[:, 1, 0:1], small[:, 1, 1:2], ALU.mult))
            cr(v.tensor_scalar(diag[:, 0, :], ident, small[:, 1, 2:3], None, ALU.mult), wait=False)
            cr(v.tensor_scalar(diag[:, 1, :], ident, small[:, 1, 0:1], None, ALU.mult), wait=False)
            assert r[0] == CR_DIAG
            v.wait_ge(s_crm, 1)
            cr(v.tensor_copy(rowa, bank[5][:, 0:P]), wait=False)
            cr(v.tensor_copy(rowc, bank[5][:, P:2 * P]), wait=False)
            cr(v.memset(bT[:, :, 0:1], 0.0))
            for q in range(DC):
                cr(v.tensor_tensor(bT[:, q, 1:P], bank[4][:, q * P:q * P + P - 1], rowc[:, 1:P], ALU.mult))
                cr(v.tensor_tensor_scan(cT[:, q, :], rowa, bT[:, q, :], 0.0, ALU.mult, ALU.max), wait=False)
            assert r[0] == CR_DONE, r[0]
            v.wait_ge(s_cr, CR_DONE + 1)
            r[0] += 1
            for i in range(3):
                cr(v.tensor_copy(carry3[:, i, :], carry[:, :]))
                if i < 2:
                    cr(v.tensor_tensor(carry[:, :], carry[:, :], carry3[:, i, :], ALU.subtract))
            assert r[0] == CR_SPLIT, r[0]

            def tile_of_x(at, t):
                return X[:, bass.ds(at + t, 1), :].rearrange("p n d -> p (n d)")

            def onehot_rows(k):
                v.tensor_tensor(oht, iota_b[:, :].unsqueeze(1).to_broadcast([P, G, P]),
                                psel[:, bass.ds(k * G, G)].unsqueeze(2).to_broadcast([P, G, P]),
                                ALU.is_equal).then_inc(s_oht, 1)

            def aggregated(k, t):
                v.wait_ge(s_end[t], 16 * k + 16)
                v.wait_ge(s_cm2, k * G + (t + 1))
                v.tensor_tensor(agg[:, t, :], end[:, t, :], bank[2 + t % 2][:, 0:D], ALU.max).then_inc(s_agg, 1)

            def graph_layer(k, t):
                xt = tile_of_x(k * G, t)
                v.wait_ge(s_my, k * G + (t + 1))
                v.tensor_tensor(xt, xt, bank[6 + t % 2][:, 0:D], ALU.add).then_inc(s_x2, 1)

            def normalized(k, t):
                v.tensor_scalar(xin[:, t, :], tile_of_x(k * G, t), mv2[:, t, 0:1], rs2[:, t:t + 1],
                                ALU.subtract, ALU.mult).then_inc(s_xin, 1)

            def scale2(k):
                v.wait_ge(s_sd2, k + 1)
                v.reciprocal(rs2, sd2).then_inc(s_rs2, 1)

            def scale3(k):
                v.wait_ge(s_sd3, k + 1)
                v.reciprocal(rs3, sd3).then_inc(s_rs3, 1)
                v.wait_ge(s_rs3, k + 1)
                v.scalar_tensor_tensor(out=nb3, in0=mv3[:, :, 0], scalar=-1.0, in1=rs3, op0=ALU.mult,
                                       op1=ALU.mult).then_inc(s_nb3, 1)

            def tiles_of(back, front, routed=None, par=None):
                if back is not None:
                    v.wait_ge(s_rs2, back + 1)
                if routed is not None:
                    v.wait_ge(s_row, routed * (G + 1) + G)
                    c = RouterSteps(v, routed, RANKS_OUT)
                for t in range(G + 4):
                    if has_place(back, t, 0):
                        normalized(back, t)
                    if has_place(front, t, 0):
                        aggregated(front, t)
                    if routed is not None:
                        weights_and_rows(v, c, par, t)
                    if back is not None and front is not None and t == 1:
                        onehot_rows(back + 2)
                    if has_place(back, t, 1):
                        stats(v, xin[:, t - 1, :], s_xin, st3, s_bn3, back * G, t - 1)
                    if has_place(front, t, 3):
                        graph_layer(front, t - 3)
                    if has_place(front, t, 4):
                        stats(v, tile_of_x(front * G, t - 4), s_x2, st2, s_bn2, front * G, t - 4)
                    if back is not None and t == G:
                        aggregate(v, st3, mv3, s_bn3, s_mv3, back * G)
                if front is not None:
                    aggregate(v, st2, mv2, s_bn2, s_mv2, front * G)

            def groups(k, routed, par=None):
                tiles_of(k, k + 1, routed, par)
                scale3(k)
                top_two(v, k)
                scale2(k + 1)
                ranks_out(v, k)

            onehot_rows(0)
            v.wait_ge(s_hist[0], 16 * GTURNS)
            v.wait_ge(s_hist[1], 16 * GTURNS)
            v.wait_ge(s_wst, 16 * E)
            v.tensor_copy(run[:, :], cst[:, C_EBASE:C_EBASE + E]).then_inc(s_padr, 1)
            v.memset(padrow, 0.0).then_inc(s_padr, 1)
            v.wait_ge(s_padr, 2)
            for s in range(2):
                v.tensor_copy(padrow[:, s, D:D + 1].bitcast(I32), cst[:, C_PADID:C_PADID + 1]).then_inc(s_padr, 1)
            tiles_of(None, 0)
            scale2(0)
            onehot_rows(1)
            groups(0, None)
            with v.Fori(0, (NG - 3) // 2) as j:
                for par in range(2):
                    groups(2 * j + par + 1, 2 * j + par, par)
            groups(NG - 2, NG - 3, 0)
            tiles_of(NG - 1, None, NG - 2, 1)
            scale3(NG - 1)
            top_two(v, NG - 1)
            ranks_out(v, NG - 1)
            tiles_of(None, None, NG - 1, 0)

            f = [0]

            def ft(ins):
                f[0] += 1
                ins.then_inc(s_ftab, 1)
                v.wait_ge(s_ftab, f[0])

            tiles, upto, ge = rv[0], rv[1], w56
            t8 = small[:, 0, 0:E]
            c8 = small[:, 1, 0:E]
            fx, fy = small[:, 2:4, :].rearrange("p a n -> p (a n)")[:, 0:FTILES], \
                small[:, 4:6, :].rearrange("p a n -> p (a n)")[:, 0:FTILES]
            v.wait_ge(s_route, 1 + NG * ROUTE_STEPS)
            ft(v.tensor_tensor(t8, run[:, :], cst[:, C_EBASE:C_EBASE + E], ALU.subtract))
            ft(v.tensor_scalar(t8, t8, FT - 0.5, 1.0 / FT, ALU.add, ALU.mult))
            ft(v.tensor_scalar(t8, t8, -0.5, ROUND, ALU.add, ALU.add))
            ft(v.tensor_scalar(t8, t8, ROUND, None, ALU.subtract))
            ft(v.tensor_tensor_scan(c8, ones[:, 0:E], t8, 0.0, ALU.mult, ALU.add))
            for e in range(E):
                ft(v.tensor_scalar(ge[:, e, :], cst[:, C_TILE:C_TILE + FTILES], c8[:, e:e + 1], None, ALU.is_ge))
            ft(v.tensor_reduce(fx, ge[:, :, :].rearrange("p e t -> p t e"), AX.X, ALU.add))
            for e in range(E):
                ft(v.tensor_scalar(ge[:, e, :], ge[:, e, :], t8[:, e:e + 1], None, ALU.mult))
            ft(v.tensor_reduce(fy, ge[:, :, :].rearrange("p e t -> p t e"), AX.X, ALU.add))
            ft(v.tensor_tensor(fy, cst[:, C_TILE:C_TILE + FTILES], fy, ALU.subtract))
            ft(v.tensor_scalar(fy, fy, float(FT), None, ALU.mult))
            ft(v.scalar_tensor_tensor(out=fy, in0=fx, scalar=float(REGION), in1=fy, op0=ALU.mult, op1=ALU.add))
            ft(v.tensor_scalar(ftab[:, 1, :], fy[0:1, :], float(E * REGION), None, ALU.min))
            ft(v.tensor_scalar(ftab[:, 0, :], fx[0:1, :], float(E - 1), None, ALU.min))
            ft(v.tensor_copy(ctab[:, :], run[0:1, :]))
            assert f[0] == FTAB_STEPS, f[0]

            def split_inputs(k, b):
                j = k * XB + b
                v.wait_ge(s_xe, 1 + DC * j + DC)
                v.tensor_copy(xeh, xe).then_inc(s_xh, 1)
                v.wait_ge(s_xh, j + 1)
                v.tensor_tensor(xel, xe, xeh, ALU.subtract).then_inc(s_xl, 1)

            def split_hidden(k, b):
                j = k * XB + b
                for q in range(HC // 2):
                    a, hq, lq = (z[:, 2 * q:2 * q + 2, :] for z in (hf, hh, hl))
                    v.wait_ge(s_gelu, HC * j + (2 * q + 2))
                    v.tensor_copy(hq, a).then_inc(s_hh, 1)
                    v.wait_ge(s_hh, (HC // 2) * j + (q + 1))
                    v.tensor_tensor(lq, a, hq, ALU.subtract).then_inc(s_hl, 1)

            def results(k, b, first=False):
                j = k * XB + b
                for s in range(SUB):
                    v.wait_ge(s_g2, SUB * j + (s + 1))
                    v.scalar_tensor_tensor(out=yt[:, s, :], in0=bank[5 + s][:, 0:D], scalar=1.0 / WS,
                                           in1=pk[b][:, PK_B2:PK_B2 + D], op0=ALU.mult,
                                           op1=ALU.add).then_inc(s_yt, 1)
                if not first:
                    v.wait_ge(s_add, 16 * SUB * j)
                for s in range(SUB):
                    v.wait_ge(s_yt, 1 + SUB * j + (s + 1))
                    v.tensor_scalar(yw[:, s, :], yt[:, s, :], xs[b][:, s, D + 1:D + 2], None,
                                    ALU.mult).then_inc(s_yw, 1)

            split_inputs(0, 0)
            for b in range(XB):
                split_hidden(0, b)
                split_inputs((b + 1) // XB, (b + 1) % XB)
                results(0, b, first=b == 0)
            with v.Fori(1, FTILES // XB - 1) as k:
                for b in range(XB):
                    split_hidden(k, b)
                    split_inputs(k + (b + 1) // XB, (b + 1) % XB)
                    results(k, b)
            for b in range(XB):
                split_hidden(FTILES // XB - 1, b)
                if b + 1 < XB:
                    split_inputs(FTILES // XB - 1, b + 1)
                results(FTILES // XB - 1, b)


_INS = ["x", "src", "dst", "fc", "fc_b", "w_bot", "wr", "br", "params", "w1", "w2", "const"]


def lay_out(i):
    import numpy as np

    a = {k: np.asarray(v) for k, v in i.items()}
    wm = a["L0_gnn_weights_matrix"]
    params = np.concatenate([
        a["L0_ffn_ln_g"].reshape(E, DC, P).transpose(0, 2, 1),
        a["L0_ffn_ln_b"].reshape(E, DC, P).transpose(0, 2, 1),
        a["L0_ffn_b1"].reshape(E, HC, P).transpose(0, 2, 1),
        np.broadcast_to(a["L0_ffn_b2"][:, None, :], (E, P, D)),
    ], axis=2)
    return {
        "x": a["x"], "src": a["src"], "dst": a["dst"],
        "fc": np.concatenate([a["L0_gnn_fc_w"], wm[0:D]], axis=1),
        "fc_b": a["L0_gnn_fc_b"][None],
        "w_bot": np.ascontiguousarray(wm[D:2 * D]),
        "wr": a["L0_ffn_Wr"], "br": np.ascontiguousarray(np.broadcast_to(a["L0_ffn_br"], (P, E))),
        "params": np.ascontiguousarray(params),
        "w1": a["L0_ffn_W1"], "w2": a["L0_ffn_W2"],
        "const": constants(),
    }


def kernel(**inputs):
    import concourse.bacc as _bacc
    from concourse import mybir as _mybir
    from concourse.bass_utils import run_bass_kernel_spmd as _run

    laid = lay_out(inputs)
    nc = _bacc.Bacc("TRN2", target_bir_lowering=False, num_devices=1)
    args = [nc.dram_tensor(f"in_{n}", laid[n].shape, _mybir.dt.from_np(laid[n].dtype), kind="ExternalInput").ap()
            for n in _INS]
    args.append(nc.dram_tensor("out_x", (ACC_ROWS, D), F32, kind="ExternalOutput").ap())
    gnn_moe_kernel(nc, *args)
    r = _run(nc, [{f"in_{n}": laid[n] for n in _INS}], core_ids=[0])
    return r.results[0]["out_x"][0:N_NODES]
```
